# Optimizing a Trainium2 kernel written in Bass

```python
import numpy as np
import jax
import jax.numpy as jnp

def _softmax(x, axis=-1):
    return jax.nn.softmax(x, axis=axis)

def _gelu(x):
    return jax.nn.gelu(x, approximate=True)

def _silu(x):
    return jax.nn.silu(x)

def _sigmoid(x):
    return jax.nn.sigmoid(x)

def _layernorm(x, axis=-1, eps=1e-05):
    m = jnp.mean(x, axis=axis, keepdims=True)
    v = jnp.var(x, axis=axis, keepdims=True)
    return (x - m) / jnp.sqrt(v + eps)

def _scatter_add(tgt, idx, src, axis=0):
    return tgt.at[idx].add(src)

def _segment_sum(src, seg, n):
    return jax.ops.segment_sum(src, seg, n)
kernel_name = 'mk_prb_d1_jaxref_r2_11588b'

def setup_inputs(seed: int=0):
    np.random.seed(seed)
    _w = jnp.asarray

    def _L0_attn_setup():
        import jax, jax.numpy as jnp
        import numpy as np
        CHUNK = 32
        H = 4

        def silu(x):
            return x * jax.nn.sigmoid(x)

        def l2norm(x):
            return x * jax.lax.rsqrt(jnp.sum(x * x, -1, keepdims=True) + 1e-06)

        def dwconv_causal(x_cl, w):
            k = w.shape[1]
            xp = jnp.pad(x_cl, ((0, 0), (0, 0), (k - 1, 0)))
            return jax.lax.conv_general_dilated(xp, w[:, None, :], (1,), 'VALID', dimension_numbers=('NCH', 'OIH', 'NCH'), feature_group_count=x_cl.shape[1])

        def short_conv_silu(x_bld, w):
            y = dwconv_causal(jnp.swapaxes(x_bld, 1, 2), w)
            return silu(jnp.swapaxes(y, 1, 2))

        def delta_rule_chunkwise(q, k, v, beta, chunk=CHUNK):
            b, h, L, dk = q.shape
            dv = v.shape[-1]
            pad = -L % chunk
            if pad:
                q, k, v = (jnp.pad(t, ((0, 0), (0, 0), (0, pad), (0, 0))) for t in (q, k, v))
                beta = jnp.pad(beta, ((0, 0), (0, 0), (0, pad)))
            n = (L + pad) // chunk
            q = l2norm(q)
            k = l2norm(k)
            v = v * beta[..., None]
            kb = k * beta[..., None]
            ch = lambda x: x.reshape(b, h, n, chunk, x.shape[-1])
            qc, kc, vc, kbc = map(ch, (q, k, v, kb))
            idx = jnp.arange(chunk)
            strict_lower = (idx[:, None] > idx[None, :]).astype(q.dtype)
            incl_lower = (idx[:, None] >= idx[None, :]).astype(q.dtype)
            attn = -jnp.einsum('bhncd,bhned->bhnce', kbc, kc) * strict_lower
            for i in range(1, chunk):
                upd = jnp.einsum('...j,...ji->...i', attn[..., i, :], attn[..., :, :i])
                attn = attn.at[..., i, :i].add(upd)
            attn = attn + jnp.eye(chunk, dtype=q.dtype)
            u = attn @ vc
            w = attn @ kbc
            xs = tuple((jnp.moveaxis(t, 2, 0) for t in (qc, kc, u, w)))
            S0 = jnp.zeros((b, h, dk, dv), q.dtype)

            def step(S, x):
                qi, ki, ui, wi = x
                a_loc = jnp.einsum('bhcd,bhed->bhce', qi, ki) * incl_lower
                ui = ui - wi @ S
                oi = qi @ S + a_loc @ ui
                S = S + jnp.einsum('bhcd,bhcv->bhdv', ki, ui)
                return (S, oi)
            S, o = jax.lax.scan(step, S0, xs)
            o = jnp.moveaxis(o, 0, 2).reshape(b, h, n * chunk, dv)[:, :, :L]
            return (o, S)

        def multiscale_conv(v, ms_w3, ms_w15, ms_w31, kernel_mix_w, channel_mixer_w):
            b, l, h, d = v.shape
            x = jnp.swapaxes(v.reshape(b, l, h * d), 1, 2)
            outs = [dwconv_causal(x, w) for w in (ms_w3, ms_w15, ms_w31)]
            y = jnp.concatenate(outs, axis=1)
            y = y.reshape(b, h, 3 * d, l).transpose(0, 3, 1, 2)
            y = y @ kernel_mix_w
            y = (y.reshape(b, l, h * d) @ channel_mixer_w).reshape(b, l, h, d)
            return y

        def _forward(hidden_states, Wq, Wk, Wv, Wb, conv_q_w, conv_k_w, conv_v_w, ms_w3, ms_w15, ms_w31, kernel_mix_w, channel_mixer_w, fusion_w1, fusion_b1, fusion_w2, fusion_b2, o_norm_w, Wo):
            b, L, D = hidden_states.shape
            h = H
            dk = Wq.shape[1] // h
            dv = Wv.shape[1] // h
            q = short_conv_silu(hidden_states @ Wq, conv_q_w).reshape(b, L, h, dk)
            k = short_conv_silu(hidden_states @ Wk, conv_k_w).reshape(b, L, h, dk)
            v = short_conv_silu(hidden_states @ Wv, conv_v_w).reshape(b, L, h, dv)
            v_direct = v
            beta = jax.nn.sigmoid(hidden_states @ Wb)
            tr = lambda x: jnp.swapaxes(x, 1, 2)
            delta_out, _S = delta_rule_chunkwise(tr(q), tr(k), tr(v), tr(beta))
            delta_out = jnp.swapaxes(delta_out, 1, 2)
            ms_out = multiscale_conv(v_direct, ms_w3, ms_w15, ms_w31, kernel_mix_w, channel_mixer_w)
            bn = lambda x: jnp.mean(jnp.abs(x), -1)
            gate_features = jnp.concatenate([hidden_states, bn(ms_out), bn(delta_out), bn(v_direct)], -1)
            hdn = jax.nn.gelu(gate_features @ fusion_w1 + fusion_b1, approximate=False)
            logits = (hdn @ fusion_w2 + fusion_b2).reshape(b, L, h, 3)
            wts = jax.nn.softmax(logits, -1)
            o = wts[..., 0:1] * ms_out + wts[..., 1:2] * delta_out + wts[..., 2:3] * v_direct
            o = o * jax.lax.rsqrt(jnp.mean(o * o, -1, keepdims=True) + 1e-05) * o_norm_w
            return o.reshape(b, L, h * dv) @ Wo
        B, L, D = (4, 1024, 512)
        h, d = (H, D // H)
        key = jax.random.key(seed)
        ks = jax.random.split(key, 20)
        nrm = lambda k, shp, s: jax.random.normal(k, shp, dtype=jnp.float32) * s
        inp = {'hidden_states': nrm(ks[0], (B, L, D), 1.0), 'Wq': nrm(ks[1], (D, D), D ** (-0.5)), 'Wk': nrm(ks[2], (D, D), D ** (-0.5)), 'Wv': nrm(ks[3], (D, D), D ** (-0.5)), 'Wb': nrm(ks[4], (D, h), D ** (-0.5)), 'conv_q_w': nrm(ks[5], (D, 4), 0.3), 'conv_k_w': nrm(ks[6], (D, 4), 0.3), 'conv_v_w': nrm(ks[7], (D, 4), 0.3), 'ms_w3': nrm(ks[8], (D, 3), 0.02), 'ms_w15': nrm(ks[9], (D, 15), 0.02), 'ms_w31': nrm(ks[10], (D, 31), 0.02), 'kernel_mix_w': nrm(ks[11], (3 * d, d), (3 * d) ** (-0.5)), 'channel_mixer_w': nrm(ks[12], (D, D), D ** (-0.5)), 'fusion_w1': nrm(ks[13], (D + 3 * h, 2 * D), (D + 3 * h) ** (-0.5)), 'fusion_b1': jnp.zeros((2 * D,), jnp.float32), 'fusion_w2': nrm(ks[14], (2 * D, 3 * h), (2 * D) ** (-0.5)), 'fusion_b2': jnp.concatenate([jnp.zeros((2 * h,), jnp.float32), jnp.ones((h,), jnp.float32)]), 'o_norm_w': jnp.ones((d,), jnp.float32), 'Wo': nrm(ks[15], (D, D), D ** (-0.5))}
        return inp
    _L0_attn_in = _L0_attn_setup()

    def _L0_ffn_setup():
        import jax, jax.numpy as jnp
        import numpy as np
        DIM = 512

        def _reference_tuple_inner(x, W_r, W_k, W_v, mu_r, mu_k):
            B, T, C = x.shape
            x_prev = jnp.concatenate([jnp.zeros((B, 1, C), x.dtype), x[:, :-1, :]], axis=1)
            xr = mu_r * x + (1.0 - mu_r) * x_prev
            xk = mu_k * x + (1.0 - mu_k) * x_prev
            r = jax.nn.sigmoid(jnp.einsum('btc,dc->btd', xr, W_r))
            k = jnp.einsum('btc,dc->btd', xk, W_k)
            k_act = jnp.square(jax.nn.relu(k))
            out = r * jnp.einsum('btc,dc->btd', k_act, W_v)
            new_state = x[:, -1, :]
            return (out, new_state)
        key = jax.random.key(seed)
        ks = jax.random.split(key, 6)
        B, T, C = (8, 1024, DIM)
        x = jax.random.normal(ks[0], (B, T, C), dtype=jnp.float32)
        s = 1.0 / np.sqrt(C)
        W_r = jax.random.uniform(ks[1], (C, C), jnp.float32, -s, s)
        W_k = jax.random.uniform(ks[2], (C, C), jnp.float32, -s, s)
        W_v = jax.random.uniform(ks[3], (C, C), jnp.float32, -s, s)
        mu_r = jax.random.uniform(ks[4], (C,), jnp.float32)
        mu_k = jax.random.uniform(ks[5], (C,), jnp.float32)
        return {'x': x, 'W_r': W_r, 'W_k': W_k, 'W_v': W_v, 'mu_r': mu_r, 'mu_k': mu_k}
    _L0_ffn_in = _L0_ffn_setup()
    _d = {'L0_attn_hidden_states': _L0_attn_in['hidden_states'], 'L0_attn_Wq': _L0_attn_in['Wq'], 'L0_attn_Wk': _L0_attn_in['Wk'], 'L0_attn_Wv': _L0_attn_in['Wv'], 'L0_attn_Wb': _L0_attn_in['Wb'], 'L0_attn_conv_q_w': _L0_attn_in['conv_q_w'], 'L0_attn_conv_k_w': _L0_attn_in['conv_k_w'], 'L0_attn_conv_v_w': _L0_attn_in['conv_v_w'], 'L0_attn_ms_w3': _L0_attn_in['ms_w3'], 'L0_attn_ms_w15': _L0_attn_in['ms_w15'], 'L0_attn_ms_w31': _L0_attn_in['ms_w31'], 'L0_attn_kernel_mix_w': _L0_attn_in['kernel_mix_w'], 'L0_attn_channel_mixer_w': _L0_attn_in['channel_mixer_w'], 'L0_attn_fusion_w1': _L0_attn_in['fusion_w1'], 'L0_attn_fusion_b1': _L0_attn_in['fusion_b1'], 'L0_attn_fusion_w2': _L0_attn_in['fusion_w2'], 'L0_attn_fusion_b2': _L0_attn_in['fusion_b2'], 'L0_attn_o_norm_w': _L0_attn_in['o_norm_w'], 'L0_attn_Wo': _L0_attn_in['Wo'], 'L0_ffn_W_r': _L0_ffn_in['W_r'], 'L0_ffn_W_k': _L0_ffn_in['W_k'], 'L0_ffn_W_v': _L0_ffn_in['W_v'], 'L0_ffn_mu_r': _L0_ffn_in['mu_r'], 'L0_ffn_mu_k': _L0_ffn_in['mu_k']}
    _x0 = _d['L0_attn_hidden_states']
    _d['L0_attn_hidden_states'] = jax.random.normal(jax.random.fold_in(jax.random.key(seed), 1), (2, 4096, 512), dtype=_x0.dtype)
    del _x0
    return _d

def reference(L0_attn_hidden_states, L0_attn_Wq, L0_attn_Wk, L0_attn_Wv, L0_attn_Wb, L0_attn_conv_q_w, L0_attn_conv_k_w, L0_attn_conv_v_w, L0_attn_ms_w3, L0_attn_ms_w15, L0_attn_ms_w31, L0_attn_kernel_mix_w, L0_attn_channel_mixer_w, L0_attn_fusion_w1, L0_attn_fusion_b1, L0_attn_fusion_w2, L0_attn_fusion_b2, L0_attn_o_norm_w, L0_attn_Wo, L0_ffn_W_r, L0_ffn_W_k, L0_ffn_W_v, L0_ffn_mu_r, L0_ffn_mu_k):

    def _L0_attn_ref(hidden_states, Wq, Wk, Wv, Wb, conv_q_w, conv_k_w, conv_v_w, ms_w3, ms_w15, ms_w31, kernel_mix_w, channel_mixer_w, fusion_w1, fusion_b1, fusion_w2, fusion_b2, o_norm_w, Wo):
        import jax, jax.numpy as jnp
        import numpy as np
        CHUNK = 32
        H = 4

        def silu(x):
            return x * jax.nn.sigmoid(x)

        def l2norm(x):
            return x * jax.lax.rsqrt(jnp.sum(x * x, -1, keepdims=True) + 1e-06)

        def dwconv_causal(x_cl, w):
            k = w.shape[1]
            xp = jnp.pad(x_cl, ((0, 0), (0, 0), (k - 1, 0)))
            return jax.lax.conv_general_dilated(xp, w[:, None, :], (1,), 'VALID', dimension_numbers=('NCH', 'OIH', 'NCH'), feature_group_count=x_cl.shape[1])

        def short_conv_silu(x_bld, w):
            y = dwconv_causal(jnp.swapaxes(x_bld, 1, 2), w)
            return silu(jnp.swapaxes(y, 1, 2))

        def delta_rule_chunkwise(q, k, v, beta, chunk=CHUNK):
            b, h, L, dk = q.shape
            dv = v.shape[-1]
            pad = -L % chunk
            if pad:
                q, k, v = (jnp.pad(t, ((0, 0), (0, 0), (0, pad), (0, 0))) for t in (q, k, v))
                beta = jnp.pad(beta, ((0, 0), (0, 0), (0, pad)))
            n = (L + pad) // chunk
            q = l2norm(q)
            k = l2norm(k)
            v = v * beta[..., None]
            kb = k * beta[..., None]
            ch = lambda x: x.reshape(b, h, n, chunk, x.shape[-1])
            qc, kc, vc, kbc = map(ch, (q, k, v, kb))
            idx = jnp.arange(chunk)
            strict_lower = (idx[:, None] > idx[None, :]).astype(q.dtype)
            incl_lower = (idx[:, None] >= idx[None, :]).astype(q.dtype)
            attn = -jnp.einsum('bhncd,bhned->bhnce', kbc, kc) * strict_lower
            for i in range(1, chunk):
                upd = jnp.einsum('...j,...ji->...i', attn[..., i, :], attn[..., :, :i])
                attn = attn.at[..., i, :i].add(upd)
            attn = attn + jnp.eye(chunk, dtype=q.dtype)
            u = attn @ vc
            w = attn @ kbc
            xs = tuple((jnp.moveaxis(t, 2, 0) for t in (qc, kc, u, w)))
            S0 = jnp.zeros((b, h, dk, dv), q.dtype)

            def step(S, x):
                qi, ki, ui, wi = x
                a_loc = jnp.einsum('bhcd,bhed->bhce', qi, ki) * incl_lower
                ui = ui - wi @ S
                oi = qi @ S + a_loc @ ui
                S = S + jnp.einsum('bhcd,bhcv->bhdv', ki, ui)
                return (S, oi)
            S, o = jax.lax.scan(step, S0, xs)
            o = jnp.moveaxis(o, 0, 2).reshape(b, h, n * chunk, dv)[:, :, :L]
            return (o, S)

        def multiscale_conv(v, ms_w3, ms_w15, ms_w31, kernel_mix_w, channel_mixer_w):
            b, l, h, d = v.shape
            x = jnp.swapaxes(v.reshape(b, l, h * d), 1, 2)
            outs = [dwconv_causal(x, w) for w in (ms_w3, ms_w15, ms_w31)]
            y = jnp.concatenate(outs, axis=1)
            y = y.reshape(b, h, 3 * d, l).transpose(0, 3, 1, 2)
            y = y @ kernel_mix_w
            y = (y.reshape(b, l, h * d) @ channel_mixer_w).reshape(b, l, h, d)
            return y

        def _forward(hidden_states, Wq, Wk, Wv, Wb, conv_q_w, conv_k_w, conv_v_w, ms_w3, ms_w15, ms_w31, kernel_mix_w, channel_mixer_w, fusion_w1, fusion_b1, fusion_w2, fusion_b2, o_norm_w, Wo):
            b, L, D = hidden_states.shape
            h = H
            dk = Wq.shape[1] // h
            dv = Wv.shape[1] // h
            q = short_conv_silu(hidden_states @ Wq, conv_q_w).reshape(b, L, h, dk)
            k = short_conv_silu(hidden_states @ Wk, conv_k_w).reshape(b, L, h, dk)
            v = short_conv_silu(hidden_states @ Wv, conv_v_w).reshape(b, L, h, dv)
            v_direct = v
            beta = jax.nn.sigmoid(hidden_states @ Wb)
            tr = lambda x: jnp.swapaxes(x, 1, 2)
            delta_out, _S = delta_rule_chunkwise(tr(q), tr(k), tr(v), tr(beta))
            delta_out = jnp.swapaxes(delta_out, 1, 2)
            ms_out = multiscale_conv(v_direct, ms_w3, ms_w15, ms_w31, kernel_mix_w, channel_mixer_w)
            bn = lambda x: jnp.mean(jnp.abs(x), -1)
            gate_features = jnp.concatenate([hidden_states, bn(ms_out), bn(delta_out), bn(v_direct)], -1)
            hdn = jax.nn.gelu(gate_features @ fusion_w1 + fusion_b1, approximate=False)
            logits = (hdn @ fusion_w2 + fusion_b2).reshape(b, L, h, 3)
            wts = jax.nn.softmax(logits, -1)
            o = wts[..., 0:1] * ms_out + wts[..., 1:2] * delta_out + wts[..., 2:3] * v_direct
            o = o * jax.lax.rsqrt(jnp.mean(o * o, -1, keepdims=True) + 1e-05) * o_norm_w
            return o.reshape(b, L, h * dv) @ Wo
        return _forward(hidden_states, Wq, Wk, Wv, Wb, conv_q_w, conv_k_w, conv_v_w, ms_w3, ms_w15, ms_w31, kernel_mix_w, channel_mixer_w, fusion_w1, fusion_b1, fusion_w2, fusion_b2, o_norm_w, Wo)

    def _L0_ffn_ref(x, W_r, W_k, W_v, mu_r, mu_k):
        import jax, jax.numpy as jnp
        import numpy as np
        DIM = 512

        def _reference_tuple_inner(x, W_r, W_k, W_v, mu_r, mu_k):
            B, T, C = x.shape
            x_prev = jnp.concatenate([jnp.zeros((B, 1, C), x.dtype), x[:, :-1, :]], axis=1)
            xr = mu_r * x + (1.0 - mu_r) * x_prev
            xk = mu_k * x + (1.0 - mu_k) * x_prev
            r = jax.nn.sigmoid(jnp.einsum('btc,dc->btd', xr, W_r))
            k = jnp.einsum('btc,dc->btd', xk, W_k)
            k_act = jnp.square(jax.nn.relu(k))
            out = r * jnp.einsum('btc,dc->btd', k_act, W_v)
            new_state = x[:, -1, :]
            return (out, new_state)
        return _reference_tuple_inner(x, W_r, W_k, W_v, mu_r, mu_k)[0]
    x = L0_attn_hidden_states
    xn = _layernorm(x, axis=-1)
    x = x + _L0_attn_ref(xn, L0_attn_Wq, L0_attn_Wk, L0_attn_Wv, L0_attn_Wb, L0_attn_conv_q_w, L0_attn_conv_k_w, L0_attn_conv_v_w, L0_attn_ms_w3, L0_attn_ms_w15, L0_attn_ms_w31, L0_attn_kernel_mix_w, L0_attn_channel_mixer_w, L0_attn_fusion_w1, L0_attn_fusion_b1, L0_attn_fusion_w2, L0_attn_fusion_b2, L0_attn_o_norm_w, L0_attn_Wo) + _L0_ffn_ref(xn, L0_ffn_W_r, L0_ffn_W_k, L0_ffn_W_v, L0_ffn_mu_r, L0_ffn_mu_k)
    return x

_drawn_inputs = setup_inputs


def setup_inputs(seed=0):
    import zlib

    import numpy as np

    out = dict(_drawn_inputs(seed))
    spreads = {'L0_attn_fusion_b1': (0.0, 0.344), 'L0_attn_o_norm_w': (1.0, 0.2)}
    factors = {'L0_attn_ms_w3': 3.314, 'L0_ffn_W_r': 4.475, 'L0_ffn_mu_r': 8.0}
    for name, (base, spread) in spreads.items():
        noise = np.random.default_rng([zlib.crc32(name.encode()), seed]).standard_normal(out[name].shape)
        drawn = base * np.exp(spread * noise) if base else spread * noise
        out[name] = jnp.asarray(drawn.astype(out[name].dtype))
    for name, factor in factors.items():
        out[name] = (out[name] * factor).astype(out[name].dtype)
    return out
```

```python
from contextlib import ExitStack

import concourse.bass as bass
from concourse import mybir

F32 = mybir.dt.float32
ALU = mybir.AluOpType
ACT = mybir.ActivationFunctionType
AX = mybir.AxisListType

P = 128
H = 4
D = H * P
NB = 2
W = NB * P
CB = D // P
HID = 2 * D
HB = HID // P
TAPS = (3, 15, 31)
SK = 4
SH = SK - 1
VH = max(TAPS) - 1
NF = 3 * H
LEVELS = [1 << i for i in range(7)]
WOFF = [0, TAPS[0] * CB, (TAPS[0] + TAPS[1]) * CB]
C_UP, C_UPI, C_ID, C_ONE = len(LEVELS), len(LEVELS) + 1, len(LEVELS) + 2, (len(LEVELS) + 3) * P


class Event:

    def __init__(self, sem, n):
        self.sem, self.n, self.seen = sem, n, 0

    def at(self, s, i):
        return s * self.n + i + 1

    def by(self, ins):
        self.seen += 1
        ins.then_inc(self.sem, 1)


def need(e, ev, s, i=None):
    if isinstance(s, int) and s < 0:
        return
    e.wait_ge(ev.sem, ev.at(s, ev.n - 1 if i is None else i))


class Schedule:

    def __init__(self):
        self.items = []
        self.group = []

    def window(self, a, b):
        self.flush()
        self.a, self.b = a, b

    def add(self, eng, cost, fn):
        self.group.append((eng, cost, fn))

    def flush(self):
        total, t = sum(c for _, c, _ in self.group), 0.0
        for eng, c, fn in self.group:
            self.items.append((self.a + (self.b - self.a) * t / total, eng, fn))
            t += c
        self.group = []

    def order(self, eng):
        return sorted(((p, fn) for p, k, fn in self.items if k == eng), key=lambda t: t[0])


def build(nc, x, out, w):
    NS = x.shape[1] // P
    with ExitStack() as ctx:
        def sb(name, *shape):
            return ctx.enter_context(nc.sbuf_tensor(name, list(shape), F32))

        def bank(name):
            return ctx.enter_context(nc.psum_tensor(name, [P, 512], F32))

        def event(name, n):
            ev = Event(ctx.enter_context(nc.semaphore(name)), n)
            events.append((name, ev))
            return ev

        events = []

        wq, wk, wv = (sb(n, P, CB, D) for n in ("wq", "wk", "wv"))
        wr, wfk, wfv = (sb(n, P, CB, D) for n in ("wr", "wfk", "wfv"))
        cm, wo = sb("cm", P, CB, D), sb("wo", P, CB, D)
        w1 = sb("w1", P, CB, HID)
        w1x = sb("w1x", NF, HID)
        km = sb("km", P, 3, P)
        w2 = sb("w2", P, HB, NF)
        b1 = sb("b1", P, HB)
        b2 = sb("b2", P, NF)
        wb = sb("wb", P, CB, H)
        onw = sb("onw", P, 1)
        mu = sb("mu", P, 2, CB)
        cw = sb("cw", P, 3, CB, SK)
        mw = sb("mw", P, sum(TAPS) * CB)
        cst = sb("cst", P, (len(LEVELS) + 3) * P + 2)
        eps = sb("eps", P, 3)
        ident = cst[:, C_ID * P:(C_ID + 1) * P]
        ones = cst[:, C_ONE:C_ONE + 1]

        def mask(i):
            return cst[:, i * P:(i + 1) * P][:, None, :].broadcast_to([P, H, P])

        xa = sb("xa", P, NB, D)
        xb = sb("xb", P, NB, D)
        xnT = sb("xnT", P, CB, W)
        xsh = sb("xsh", P, CB, NB, 1 + P)
        xr, xk = sb("xr", P, CB, W), sb("xk", P, CB, W)
        rl = sb("rl", P, 2 * W)
        ka = sb("ka", P, CB, W)
        th = sb("th", P, D)
        raw = [sb(f"raw{i}", P, 2, NB, SH + P) for i in range(2)]
        halo = sb("halo", P, 3 * CB, NB, SH)
        qT, kT = sb("qT", P, CB, W), sb("kT", P, CB, W)
        vT = sb("vT", P, CB, NB, VH + P)
        ktok, vtok = sb("ktok", P, NB, D), sb("vtok", P, NB, D)
        y, u = sb("y", P, NB, D), sb("u", P, NB, D)
        Bm, Y, X, Wm, aT = (sb(n, P, NB, D) for n in ("Bm", "Y", "X", "Wm", "aT"))
        S = sb("S", P, NB, D)
        dl = sb("dl", P, NB, D)
        my = [sb(f"my{i}", P, 3, W) for i in range(2)]
        ym = sb("ym", P, CB, W)
        ms = sb("ms", P, NB, D)
        hd = sb("hd", P, 4, W)
        bst, mv = sb("bst", P, NB, 6), sb("mv", P, NB, 2)
        std, rstd, nmr = sb("std", P, NB), sb("rstd", P, NB), sb("nmr", P, NB)
        nrm, rn = sb("nrm", P, NB, 2 * H), sb("rn", P, NB, 2 * H)
        bt, gt, g = sb("bt", P, NB, H), sb("gt", P, NB, H), sb("g", P, NB, H)
        ft, ftT = sb("ft", P, NB, NF), sb("ftT", NF, W)
        lg, gw = sb("lg", P, NB, H, 3), sb("gw", P, NB, H, 3)
        mx, sm, rs = sb("mx", P, NB * H), sb("sm", P, NB * H), sb("rs", P, NB * H)
        so, ro, rro = sb("so", P, NB, H), sb("ro", P, NB, H), sb("rro", P, NB, H)
        sq = Wm[:, :, :].rearrange("p b (c w) -> p (b c) w", w=W)

        front = [bank(f"front{i}") for i in range(2)]
        dense = [bank(f"dense{i}") for i in range(2)]
        cell = [bank(f"cell{b}") for b in range(NB)]
        turn = bank("turn")
        small = bank("small")
        s_norm = small[:, 0:NB * 2 * H]
        s_beta = small[:, 32:32 + NB * H]
        s_ft = small[0:NF, 64:64 + W]
        s_mix = small[:, 64:64 + W]
        s_lg = small[:, 384:384 + NB * NF]

        def hv(t, b):
            return t[:, b, :].rearrange("p (h d) -> p h d", h=H)

        def bh(t):
            return t[:, :].rearrange("p (h d) -> p h d", h=H)

        def wide(col):
            return col[:, :, None].broadcast_to([P, H, P])

        def hs(h):
            return slice(h * P, (h + 1) * P)

        held = ctx.enter_context(nc.semaphore("held"))

        def hold(e):
            e.sem_inc(held, 1)

        wload = ctx.enter_context(nc.semaphore("wload"))
        setup = ctx.enter_context(nc.semaphore("setup"))
        wol = ctx.enter_context(nc.semaphore("wo_scaled"))
        xa_in = ctx.enter_context(nc.semaphore("xa_in"))
        xb_in = ctx.enter_context(nc.semaphore("xb_in"))
        stored = ctx.enter_context(nc.semaphore("stored"))

        sf, sk = Schedule(), Schedule()

        e_stat, e_agg = event("e_stat", NB), event("e_agg", NB)
        e_std, e_rstd, e_nmr = event("e_std", 1), event("e_rstd", 1), event("e_nmr", 1)
        e_xn, e_xT, e_xnT = event("e_xn", NB), event("e_xT", NB), event("e_xnT", NB)
        e_proj, e_raw = event("e_proj", 6), event("e_raw", 6)
        e_hin, e_hout = event("e_hin", 6), event("e_hout", 6)
        e_vh = event("e_vh", 1)
        e_cv = event("e_cv", 6 * 2 * SK)
        e_act = event("e_act", 6)
        e_xcp = event("e_xcp", 2)
        e_msc = event("e_msc", CB * sum(TAPS))
        e_tk, e_sqk = event("e_tk", 2 * NB), event("e_sq", 2)
        e_S, e_KTu = event("e_S", NB), event("e_KTu", NB)
        e_o = event("e_o", NB)
        e_xb = event("e_xb", NB)
        e_gr, e_qk = event("e_gr", NB), event("e_qk", NB)

        sf.window(0.0, 0.05)

        def f(e, s):
            need(e, e_xT, s - 1)
            e.dma_start(xa[:, :, :], x[:, bass.ds(s * P, P), :].rearrange("b p d -> p b d")).then_inc(xa_in, 16)
        sf.add("sp", 1, f)

        sf.window(0.25, 0.27)

        def f(e, s):
            e.wait_ge(xa_in, s * 16 + 16)
            for b in range(NB):
                e_stat.by(e.bn_stats(bst[:, b, :], xa[:, b, :]))
            for b in range(NB):
                need(e, e_stat, s, b)
                if b == 0:
                    need(e, e_xn, s - 1)
                hold(e)
                e_agg.by(e.bn_aggr(mv[:, b, :], bst[:, b, :]))
        sf.add("dve", 2, f)

        def f(e, s):
            need(e, e_agg, s)
            need(e, e_rstd, s - 1)
            e_std.by(e.activation(std[:, :], mv[:, :, 1], ACT.Sqrt, bias=eps[:, 0:1]))
        sf.add("act", 1, f)

        def f(e, s):
            need(e, e_std, s)
            e_rstd.by(e.reciprocal(rstd[:, :], std[:, :]))
            need(e, e_rstd, s)
            e_nmr.by(e.scalar_tensor_tensor(nmr[:, :], mv[:, :, 0], -1.0, rstd[:, :], ALU.mult, ALU.mult))
        sf.add("dve", 1, f)

        sf.window(0.33, 0.35)
        for b in range(NB):
            def f(e, s, b=b):
                e.wait_ge(xa_in, s * 16 + 16)
                need(e, e_nmr, s)
                e_xn.by(e.activation(xa[:, b, :], xa[:, b, :], ACT.Identity, bias=nmr[:, b:b + 1],
                                     scale=rstd[:, b:b + 1]))
            sf.add("act", 1, f)

            def f(e, s, b=b):
                need(e, e_xn, s, b)
                need(e, e_raw, s - 1, 4 + b)
                for c in range(CB):
                    i = e.transpose(front[b][:, hs(c)], xa[:, b, hs(c)], ident)
                e_xT.by(i)
            sf.add("pe", 1, f)

            def f(e, s, b=b):
                need(e, e_xT, s, b)
                need(e, e_xcp, s - 1)
                need(e, e_proj, s - 1)
                e_xnT.by(e.copy(xnT[:, :, hs(b)], bh(front[b])))
            sf.add("act", 1, f)

        for pair in range(6):
            j, c0 = pair // 2, 2 * (pair % 2)
            wt, r = (wq, wk, wv)[j], raw[pair % 2]
            if pair == 0:
                sf.window(0.61, 0.79)
            if pair == 4:
                sf.window(0.81, 1.0)

            def f(e, s, pair=pair, wt=wt, c0=c0):
                if pair == 0:
                    need(e, e_xnT, s)
                if pair < 2:
                    need(e, e_xnT, s, pair)
                else:
                    need(e, e_raw, s, pair - 2)
                for c in range(2):
                    for k in range(CB):
                        i = e.matmul(front[pair % 2][:, c * W:(c + 1) * W], wt[:, k, hs(c0 + c)], xnT[:, k, :],
                                     start=(k == 0), stop=(k == CB - 1))
                e_proj.by(i)
            sf.add("pe", 2, f)

            def f(e, s, pair=pair, r=r):
                need(e, e_cv, s if pair >= 2 else s - 1, 2 * SK * ((pair - 2) % 6) + 2 * SK - 1)
                if pair == 4:
                    need(e, e_msc, s - 1)
                    need(e, e_tk, s - 1)
                    hold(e)
                    e_vh.by(e.tensor_copy(vT[:, :, :, 0:VH], vT[:, :, :, P:P + VH]))
                need(e, e_hout, s - 1, pair)
                hold(e)
                e_hin.by(e.tensor_copy(r[:, :, :, 0:SH],
                                       halo[:, 2 * pair:2 * pair + 2, :, :]))
            sf.add("pool", 1, f)

            def f(e, s, pair=pair, r=r):
                need(e, e_proj, s, pair)
                if pair >= 2:
                    need(e, e_cv, s, 2 * SK * (pair - 1) - 1)
                    need(e, e_hout, s, pair - 2)
                else:
                    need(e, e_cv, s - 1, 2 * SK * (pair + 5) - 1)
                    need(e, e_hout, s - 1, pair + 4)
                for c in range(2):
                    i = e.copy(r[:, c, :, SH:SH + P],
                               front[pair % 2][:, c * W:(c + 1) * W].rearrange("p (b t) -> p b t", b=NB))
                e_raw.by(i)
            sf.add("act", 1, f)

            def f(e, s, pair=pair, r=r):
                need(e, e_raw, s, pair)
                need(e, e_hin, s, pair)
                hold(e)
                e_hout.by(e.tensor_copy(halo[:, 2 * pair:2 * pair + 2, :, :], r[:, :, :, P:P + SH]))
            sf.add("pool", 1, f)

            def dst(c, j=j, c0=c0):
                if j == 2:
                    return vT[:, c0 + c, :, VH:VH + P]
                return (qT, kT)[j][:, c0 + c, :].rearrange("p (b t) -> p b t", b=NB)

            def f(e, s, pair=pair, r=r, j=j, c0=c0, dst=dst):
                need(e, e_raw, s, pair)
                need(e, e_hin, s, pair)
                if pair == 0:
                    need(e, e_o, s - 1)
                    need(e, e_qk, s - 1)
                    need(e, e_sqk, s - 1)
                if pair == 2:
                    need(e, e_KTu, s - 1)
                    need(e, e_tk, s - 1)
                if pair == 4:
                    need(e, e_vh, s)
                for t in range(SK):
                    for c in range(2):
                        n = 2 * SK * pair + 2 * t + c
                        src, wc = r[:, c, :, t:t + P], cw[:, j, c0 + c, t:t + 1]
                        if t == 0:
                            i = e.tensor_scalar(dst(c), src, wc, None, ALU.mult)
                        else:
                            need(e, e_cv, s, n - 2)
                            i = e.scalar_tensor_tensor(dst(c), src, wc, dst(c), ALU.mult, ALU.add)
                        e_cv.by(i)
            sf.add("dve", 8, f)

            def f(e, s, pair=pair, dst=dst):
                need(e, e_cv, s, 2 * SK * (pair + 1) - 1)
                for c in range(2):
                    i = e.activation(dst(c), dst(c), ACT.Silu)
                e_act.by(i)
            sf.add("act", 2, f)
        sf.flush()

        e_fmm, e_frl, e_ka = event("e_fmm", 2), event("e_frl", 2), event("e_ka", 2)
        e_dx, e_xrk = event("e_dx", 1), event("e_xrk", 2 * CB)
        e_r, e_th = event("e_r", NB), event("e_th", NB)
        e_kv, e_gate = event("e_kv", NB), event("e_gate", NB)
        e_res = event("e_res", NB)
        e_nn, e_bm = event("e_nn", 2), event("e_bm", 1)
        e_nrm, e_rn, e_bt, e_b2, e_gt, e_g = (event(n, 1) for n in ("e_nrm", "e_rn", "e_bt", "e_b2", "e_gt", "e_g"))
        e_tT = event("e_tT", 2 * NB)
        e_vn = event("e_vn", NB)
        e_B, e_aT = event("e_B", NB * H), event("e_aT", NB)
        NL = len(LEVELS)
        e_Wp, e_W = event("e_Wp", NB * NL), event("e_W", NB * NL)
        e_Xp, e_X = event("e_Xp", NB * NL), event("e_X", NB * NL)
        e_Zp, e_Y = event("e_Zp", NB * (NL - 1)), event("e_Y", NB * NL)
        e_KS, e_y, e_Xy, e_u = (event(n, NB) for n in ("e_KS", "e_y", "e_Xy", "e_u"))
        e_d = event("e_d", NB)
        e_km, e_ym = event("e_km", H), event("e_ym", H)
        e_cm, e_ms = event("e_cm", NB), event("e_ms", NB)
        e_ft = event("e_ft", 3 * NB)
        e_fp, e_fT = event("e_fp", NB), event("e_fT", NB)
        e_z, e_h, e_l = event("e_z", HB // 2), event("e_h", HB // 2), event("e_l", HB // 2)
        e_lb, e_mx, e_sub, e_ex, e_sm, e_rs, e_gw = (
            event(n, 1) for n in ("e_lb", "e_mx", "e_sub", "e_ex", "e_sm", "e_rs", "e_gw"))
        e_m0, e_m1, e_m2 = event("e_m0", NB), event("e_m1", NB), event("e_m2", NB)
        e_a1, e_a2 = event("e_a1", NB), event("e_a2", NB)
        e_sqo, e_so, e_ro, e_rro, e_on = (event(n, NB) for n in ("e_sqo", "e_so", "e_ro", "e_rro", "e_on"))
        e_oTp, e_oT, e_att = event("e_oTp", NB), event("e_oT", NB), event("e_att", NB)

        sk.window(0.0, 0.03)

        def f(e, s):
            if not (isinstance(s, int) and s == 0):
                e.wait_ge(stored, s * 16)
            e.dma_start(xb[:, :, :], x[:, bass.ds(s * P, P), :].rearrange("b p d -> p b d")).then_inc(xb_in, 16)
        sk.add("sp", 1, f)

        def f(e, s):
            need(e, e_act, s, 1)
            need(e, e_Zp, s - 1)
            e_sqk.by(e.tensor_tensor(sq, qT[:, :, :], qT[:, :, :], ALU.mult))
            need(e, e_act, s, 3)
            need(e, e_nn, s, 0)
            e_sqk.by(e.tensor_tensor(sq, kT[:, :, :], kT[:, :, :], ALU.mult))
        sk.add("pool", 1, f)

        def f(e, s):
            need(e, e_lb, s - 1)
            for j in range(2):
                need(e, e_sqk, s, j)
                for b in range(NB):
                    for h in range(H):
                        n = b * 2 * H + j * H + h
                        i = e.matmul(s_norm[:, n:n + 1], sq[:, h, hs(b)], ones, start=True, stop=True)
                e_nn.by(i)
        sk.add("pe", 1, f)

        def f(e, s):
            need(e, e_xnT, s)
            need(e, e_z, s - 1)
            need(e, e_xrk, s - 1)
            hold(e)
            e_xcp.by(e.tensor_copy(xsh[:, :, :, 0:1], xsh[:, :, :, P:P + 1]))
            need(e, e_xcp, s, 0)
            hold(e)
            e_xcp.by(e.tensor_copy(xsh[:, :, :, 1:1 + P], xnT[:, :, :].rearrange("p c (b t) -> p c b t", b=NB)))
        sk.add("pool", 1, f)

        def f(e, s):
            need(e, e_xcp, s)
            for b in range(NB):
                for k in range(CB):
                    i = e.matmul(s_beta[:, b * H:(b + 1) * H], xsh[:, k, b, 1:1 + P], wb[:, k, :],
                                 start=(k == 0), stop=(k == CB - 1))
            e_bm.by(i)
        sk.add("pe", 1, f)

        def f(e, s):
            need(e, e_nn, s)
            need(e, e_bm, s)
            need(e, e_d, s - 1)
            need(e, e_vn, s - 1)
            e_nrm.by(e.activation(nrm[:, :, :], s_norm.rearrange("p (b n) -> p b n", b=NB), ACT.Sqrt,
                                  bias=eps[:, 1:2]))
            need(e, e_b2, s - 1)
            e_bt.by(e.activation(bt[:, :, :], s_beta.rearrange("p (b n) -> p b n", b=NB), ACT.Tanh, scale=0.5))
        sk.add("act", 1, f)

        def f(e, s):
            need(e, e_nrm, s)
            e_rn.by(e.reciprocal(rn[:, :, :], nrm[:, :, :]))
            need(e, e_bt, s)
            e_b2.by(e.tensor_scalar(gt[:, :, :], bt[:, :, :], 0.5, 0.5, ALU.mult, ALU.add))
            need(e, e_rn, s)
            need(e, e_b2, s)
            e_gt.by(e.tensor_tensor(gt[:, :, :], gt[:, :, :], rn[:, :, H:2 * H], ALU.mult))
            need(e, e_gt, s)
            e_g.by(e.tensor_tensor(g[:, :, :], gt[:, :, :], rn[:, :, H:2 * H], ALU.mult))
        sk.add("dve", 1, f)

        sk.window(0.03, 0.1)
        for b in range(NB):
            for j, (src, tok) in enumerate(((kT, ktok), (vT, vtok))):
                n = 2 * b + j

                def f(e, s, b=b, j=j, n=n, src=src):
                    need(e, e_act, s, 3 + 2 * j)
                    if n == 0:
                        need(e, e_oT, s - 1)
                    else:
                        need(e, e_tk, s, n - 1)
                    for h in range(H):
                        t = kT[:, h, hs(b)] if j == 0 else vT[:, h, b, VH:VH + P]
                        i = e.transpose(turn[:, hs(h)], t, ident)
                    e_tT.by(i)
                sk.add("pe", 1, f)

                def f(e, s, b=b, j=j, n=n, tok=tok):
                    need(e, e_tT, s, n)
                    need(e, (e_KTu, e_m2)[j], s - 1, b)
                    if j:
                        need(e, e_ft, s - 1, 3 * b + 2)
                    e_tk.by(e.copy(tok[:, b, :], turn[:, :]))
                sk.add("act", 1, f)

            def f(e, s, b=b):
                need(e, e_tk, s, 2 * b + 1)
                need(e, e_nrm, s)
                need(e, e_Xy, s - 1, b)
                e_vn.by(e.tensor_tensor(hv(y, b), hv(vtok, b), wide(nrm[:, b, H:2 * H]), ALU.mult))
            sk.add("pool", 1, f)

            def f(e, s, b=b):
                if b == 0:
                    need(e, e_act, s, 3)
                need(e, e_S, s - 1, b)
                for h in range(H):
                    i = e.matmul(cell[b][:, hs(h)], kT[:, h, hs(b)], kT[:, h, hs(b)], start=True, stop=True)
                e_gr.by(i)
            sk.add("pe", 1, f)

            def f(e, s, b=b):
                need(e, e_gr, s, b)
                need(e, e_g, s)
                need(e, e_Wp, s - 1, NB * (NL - 1) + b)
                for h in range(H):
                    e_B.by(e.scalar_tensor_tensor(Bm[:, b, hs(h)], cell[b][:, hs(h)], g[:, b, h:h + 1],
                                                  cst[:, C_UP * P:(C_UP + 1) * P], ALU.mult, ALU.mult))
            sk.add("dve", 1, f)

        for b in range(NB):
            def f(e, s, b=b):
                need(e, e_B, s, H * (b + 1) - 1)
                for h in range(H):
                    i = e.matmul(cell[b][:, hs(h)], kT[:, h, hs(b)], qT[:, h, hs(b)], start=True, stop=True)
                e_qk.by(i)
            sk.add("pe", 1, f)

            def f(e, s, b=b):
                need(e, e_qk, s, b)
                need(e, e_o, s - 1, b)
                e_aT.by(e.tensor_tensor(hv(aT, b), bh(cell[b]), mask(C_UPI), ALU.mult))
            sk.add("dve", 1, f)

        sk.window(0.1, 0.45)
        for l in range(NL):
            for b in range(NB):
                n = NB * l + b

                def f(e, s, l=l, b=b, n=n):
                    if l == 0:
                        need(e, e_aT, s, b)
                        for h in range(H):
                            i = e.transpose(cell[b][:, hs(h)], Bm[:, b, hs(h)], ident)
                        e_Wp.by(i)
                        return
                    need(e, e_Y, s, n - NB)
                    for h in range(H):
                        i = e.matmul(cell[b][:, hs(h)], Bm[:, b, hs(h)], Y[:, b, hs(h)], start=True, stop=True)
                    e_Wp.by(i)
                    m = n - NB
                    if m == 0:
                        need(e, e_tk, s)
                    else:
                        need(e, e_X, s, m - 1)
                    for h in range(H):
                        i = e.transpose(turn[:, hs(h)], Y[:, b, hs(h)], ident)
                    e_Xp.by(i)
                sk.add("pe", 2, f)

                def f(e, s, l=l, b=b, n=n):
                    need(e, e_Wp, s, n)
                    if l == 0:
                        need(e, e_nn, s, 1)
                    e_W.by(e.tensor_tensor(hv(Wm, b), bh(cell[b]), mask(l), ALU.mult))
                sk.add("dve", 1, f)

                if l:
                    def f(e, s, b=b, n=n):
                        need(e, e_Xp, s, n - NB)
                        if n - NB < NB:
                            need(e, e_Xy, s - 1, b)
                        else:
                            need(e, e_Zp, s, n - 2 * NB)
                        e_X.by(e.copy(X[:, b, :], turn[:, :]))
                    sk.add("act", 1, f)
            for b in range(NB):
                n = NB * l + b
                if l:
                    def f(e, s, b=b, n=n):
                        need(e, e_W, s, n)
                        need(e, e_X, s, n - NB)
                        for h in range(H):
                            i = e.matmul(cell[b][:, hs(h)], X[:, b, hs(h)], Wm[:, b, hs(h)], start=True, stop=True)
                        e_Zp.by(i)
                    sk.add("pe", 2, f)

                def f(e, s, l=l, b=b, n=n):
                    if l == 0:
                        need(e, e_W, s, n)
                        if b == 0:
                            need(e, e_Xp, s - 1)
                        e_Y.by(e.tensor_tensor(hv(Y, b), mask(C_ID), hv(Wm, b), ALU.subtract))
                    else:
                        need(e, e_Zp, s, n - NB)
                        e_Y.by(e.tensor_tensor(hv(Y, b), hv(Y, b), bh(cell[b]), ALU.subtract))
                sk.add("dve", 1, f)

        sk.window(0.45, 0.6)
        for b in range(NB):
            m = NB * (NL - 1) + b

            def f(e, s, b=b, m=m):
                need(e, e_Y, s, m)
                need(e, e_X, s, m - 1)
                for h in range(H):
                    i = e.transpose(turn[:, hs(h)], Y[:, b, hs(h)], ident)
                e_Xp.by(i)
                need(e, e_S, s - 1, b)
                for h in range(H):
                    i = e.matmul(cell[b][:, hs(h)], kT[:, h, hs(b)], S[:, b, hs(h)], start=True, stop=True)
                e_KS.by(i)
            sk.add("pe", 1, f)

            def f(e, s, b=b, m=m):
                need(e, e_Xp, s, m)
                need(e, e_Zp, s, m - NB)
                e_X.by(e.copy(X[:, b, :], turn[:, :]))
            sk.add("act", 1, f)

            def f(e, s, b=b):
                need(e, e_KS, s, b)
                need(e, e_vn, s, b)
                e_y.by(e.tensor_tensor(y[:, b, :], y[:, b, :], cell[b][:, :], ALU.subtract))
            sk.add("dve", 1, f)
        for b in range(NB):
            m = NB * (NL - 1) + b

            def f(e, s, b=b, m=m):
                need(e, e_y, s, b)
                need(e, e_X, s, m)
                for h in range(H):
                    i = e.matmul(cell[b][:, hs(h)], X[:, b, hs(h)], y[:, b, hs(h)], start=True, stop=True)
                e_Xy.by(i)
            sk.add("pe", 1, f)

            def f(e, s, b=b):
                need(e, e_Xy, s, b)
                need(e, e_KTu, s - 1, b)
                e_u.by(e.tensor_tensor(hv(u, b), bh(cell[b]), wide(g[:, b, :]), ALU.mult))
            sk.add("dve", 1, f)
        for b in range(NB):
            def f(e, s, b=b):
                need(e, e_u, s, b)
                need(e, e_aT, s, b)
                for h in range(H):
                    e.matmul(cell[b][:, hs(h)], qT[:, h, hs(b)], S[:, b, hs(h)], start=True, stop=False)
                    i = e.matmul(cell[b][:, hs(h)], aT[:, b, hs(h)], u[:, b, hs(h)], start=False, stop=True)
                e_o.by(i)
            sk.add("pe", 1, f)

            def f(e, s, b=b):
                need(e, e_o, s, b)
                need(e, e_rn, s)
                need(e, e_on, s - 1, b)
                e_d.by(e.tensor_tensor(hv(dl, b), bh(cell[b]), wide(rn[:, b, 0:H]), ALU.mult))
            sk.add("dve", 1, f)
        for b in range(NB):
            def f(e, s, b=b):
                need(e, e_d, s, b)
                for h in range(H):
                    i = e.matmul(cell[b][:, hs(h)], ktok[:, b, hs(h)], u[:, b, hs(h)], start=True, stop=True)
                e_KTu.by(i)
            sk.add("pe", 1, f)

            def f(e, s, b=b):
                need(e, e_KTu, s, b)
                e_S.by(e.tensor_tensor(S[:, b, :], S[:, b, :], cell[b][:, :], ALU.add))
            sk.add("dve", 1, f)

        sk.window(0.03, 0.2)

        def f(e, s):
            need(e, e_xcp, s)
            need(e, e_fmm, s - 1)
            need(e, e_r, s - 1)
            xrv = ka[:, :, :].rearrange("p c (b t) -> p c b t", b=NB)
            need(e, e_kv, s - 1)
            e_dx.by(e.tensor_tensor(xrv, xsh[:, :, :, 1:1 + P], xsh[:, :, :, 0:P], ALU.subtract))
            need(e, e_dx, s)
            for j, dst in enumerate((xr, xk)):
                for c in range(CB):
                    e_xrk.by(e.scalar_tensor_tensor(
                        dst[:, c, :].rearrange("p (b t) -> p b t", b=NB), xrv[:, c, :, :],
                        mu[:, j, c:c + 1], xsh[:, c, :, 0:P], ALU.mult, ALU.add))
        sk.add("dve", 1, f)

        sk.window(0.15, 0.55)
        for pair in range(2):
            def f(e, s, pair=pair):
                need(e, e_xrk, s)
                need(e, e_xb, s - 1, pair)
                for c in range(2):
                    for k in range(CB):
                        i = e.matmul(dense[pair][:, c * W:(c + 1) * W], wfk[:, k, hs(2 * pair + c)], xk[:, k, :],
                                     start=(k == 0), stop=(k == CB - 1))
                e_fmm.by(i)
            sk.add("pe", 2, f)

            def f(e, s, pair=pair):
                need(e, e_fmm, s, pair)
                need(e, e_ka, s if pair else s - 1, 1 - pair if not pair else 0)
                e_frl.by(e.activation(rl[:, :], dense[pair][:, :], ACT.Relu))
            sk.add("act", 1, f)

            def f(e, s, pair=pair):
                need(e, e_frl, s, pair)
                need(e, e_xrk, s)
                e_ka.by(e.scalar_tensor_tensor(ka[:, 2 * pair:2 * pair + 2, :],
                                               rl[:, :].rearrange("p (c w) -> p c w", c=2), 0.5,
                                               rl[:, :].rearrange("p (c w) -> p c w", c=2), ALU.mult, ALU.mult))
            sk.add("dve", 1, f)
        for b in range(NB):
            def f(e, s, b=b):
                need(e, e_xrk, s)
                need(e, e_frl, s, 0) if b == 0 else need(e, e_gate, s, 0)
                for k in range(CB):
                    i = e.matmul(dense[0][:, :], xr[:, k, hs(b)], wr[:, k, :], start=(k == 0), stop=(k == CB - 1))
                e_r.by(i)
                need(e, e_ka, s)
                need(e, e_frl, s, 1) if b == 0 else need(e, e_gate, s, 0)
                for k in range(CB):
                    i = e.matmul(dense[1][:, :], ka[:, k, hs(b)], wfv[:, k, :], start=(k == 0), stop=(k == CB - 1))
                e_kv.by(i)
            sk.add("pe", 4, f)

            def f(e, s, b=b):
                need(e, e_r, s, b)
                need(e, e_res, s, 0) if b else need(e, e_res, s - 1, 1)
                e_th.by(e.activation(th[:, :], dense[0][:, :], ACT.Tanh, scale=0.5))
            sk.add("act", 1, f)

            def f(e, s, b=b):
                need(e, e_th, s, b)
                need(e, e_kv, s, b)
                e_gate.by(e.scalar_tensor_tensor(th[:, :], th[:, :], 1.0, dense[1][:, :], ALU.add, ALU.mult))
            sk.add("dve", 1, f)

            def f(e, s, b=b):
                need(e, e_gate, s, b)
                e.wait_ge(xb_in, s * 16 + 16)
                e_res.by(e.tensor_tensor(xb[:, b, :], xb[:, b, :], th[:, :], ALU.add))
            sk.add("pool", 1, f)

        step_of = {}
        n = 0
        sk.window(0.0, 0.78)
        for h in range(H):
            blocks = [((3 * h + p) // CB, (3 * h + p) % CB) for p in range(3)]
            plan = sorted((t, p) for p in range(3) for t in range(TAPS[blocks[p][0]]))
            last = {}
            ends = {}
            for t, p in plan:
                j, c = blocks[p]

                def f(e, s, h=h, t=t, p=p, j=j, c=c, prev=last.get(p), n=n):
                    if n == 0:
                        need(e, e_act, s)
                    o = my[h % 2][:, p, :].rearrange("p (b t) -> p b t", b=NB)
                    off = VH - (TAPS[j] - 1) + t
                    src = vT[:, c, :, off:off + P]
                    col = WOFF[j] + c * TAPS[j] + t
                    if prev is None:
                        if p == 0:
                            need(e, e_km, s - 1 if h < 2 else s, (h + 2) % H)
                        i = e.tensor_scalar(o, src, mw[:, col:col + 1], None, ALU.mult)
                    else:
                        need(e, e_msc, s, prev)
                        i = e.scalar_tensor_tensor(o, src, mw[:, col:col + 1], o, ALU.mult, ALU.add)
                    e_msc.by(i)
                sk.add("dve", 1, f)
                last[p] = n
                n += 1
            step_of[h] = n - 1
        for h in range(H):
            at = 0.78 * (step_of[h] + 1) / n
            sk.window(at, at + 0.02)

            def f(e, s, h=h):
                need(e, e_msc, s, step_of[h])
                need(e, e_ym if h else e_bt, s, h - 1 if h else 0)
                for p in range(3):
                    i = e.matmul(s_mix, km[:, p, :], my[h % 2][:, p, :], start=(p == 0), stop=(p == 2))
                e_km.by(i)
            sk.add("pe", 1, f)

            def f(e, s, h=h):
                need(e, e_km, s, h)
                if h == 0:
                    need(e, e_att, s - 1)
                e_ym.by(e.copy(ym[:, h, :], s_mix))
            sk.add("act", 1, f)
        sk.window(0.8, 0.83)
        for b in range(NB):
            def f(e, s, b=b):
                need(e, e_ym, s)
                need(e, (e_th, e_gate)[b], s)
                for k in range(CB):
                    i = e.matmul(dense[b][:, :], ym[:, k, hs(b)], cm[:, k, :], start=(k == 0), stop=(k == CB - 1))
                e_cm.by(i)
            sk.add("pe", 1, f)

            def f(e, s, b=b):
                need(e, e_cm, s, b)
                need(e, e_a1, s - 1, b)
                e_ms.by(e.copy(ms[:, b, :], dense[b][:, :]))
            sk.add("act", 1, f)

            def f(e, s, b=b):
                need(e, e_fp, s - 1, b)
                for j, (t, ev, i) in enumerate(((ms, e_ms, b), (dl, e_d, b), (vtok, e_tk, 2 * b + 1))):
                    need(e, ev, s, i)
                    e_ft.by(e.tensor_reduce(ft[:, b, j * H:(j + 1) * H], hv(t, b), AX.X, ALU.add,
                                            apply_absolute_value=True))
            sk.add("dve", 1, f)

            def f(e, s, b=b):
                need(e, e_ft, s, 3 * b + 2)
                e_fp.by(e.matmul(s_ft[:, hs(b)], ft[:, b, :], ident, start=True, stop=True))
            sk.add("pe", 1, f)

        def f(e, s):
            need(e, e_fp, s)
            need(e, e_z, s - 1)
            for b in range(NB):
                e_fT.by(e.activation(ftT[:, hs(b)], s_ft[:, hs(b)], ACT.Copy, scale=1.0 / P))
        sk.add("act", 1, f)

        sk.window(0.83, 0.93)
        for pair in range(HB // 2):
            def f(e, s, pair=pair):
                if pair < 2:
                    need(e, e_ms, s, pair)
                else:
                    need(e, e_h, s, pair - 2)
                need(e, e_fT, s)
                for c in range(2):
                    o = dense[pair % 2][:, c * W:(c + 1) * W]
                    for k in range(CB):
                        e.matmul(o.rearrange("p (b t) -> p b t", b=NB), w1[:, k, hs(2 * pair + c)],
                                 xsh[:, k, :, 1:1 + P], start=(k == 0), stop=False)
                    i = e.matmul(o, w1x[:, hs(2 * pair + c)], ftT[:, :], start=False, stop=True)
                e_z.by(i)
            sk.add("pe", 2, f)

            def f(e, s, pair=pair):
                need(e, e_z, s, pair)
                need(e, e_l, s if pair >= 2 else s - 1, (pair - 2) % (HB // 2))
                for c in range(2):
                    m = 2 * pair + c
                    i = e.activation(hd[:, m % 4, :], dense[pair % 2][:, c * W:(c + 1) * W], ACT.Gelu,
                                     bias=b1[:, m:m + 1])
                e_h.by(i)
            sk.add("act", 2, f)

        def logits(pair):
            def f(e, s):
                need(e, e_h, s, pair)
                for c in range(2):
                    m = 2 * pair + c
                    for b in range(NB):
                        i = e.matmul(s_lg[:, b * NF:(b + 1) * NF], hd[:, m % 4, hs(b)], w2[:, m, :],
                                     start=(m == 0 and b == 0), stop=(m == HB - 1), skip_group_check=True)
                e_l.by(i)
            return f
        sk.window(0.86, 0.94)
        for pair in range(HB // 2):
            sk.add("pe", 1, logits(pair))

        sk.window(0.93, 0.95)

        def f(e, s):
            need(e, e_l, s)
            need(e, e_gw, s - 1)
            e_lb.by(e.tensor_tensor(lg[:, :, :, :].rearrange("p b h r -> p b (h r)"),
                                    s_lg.rearrange("p (b n) -> p b n", b=NB),
                                    b2[:, None, :].broadcast_to([P, NB, NF]), ALU.add))
            l3 = lg[:, :, :, :].rearrange("p b h r -> p (b h) r")
            w3 = gw[:, :, :, :].rearrange("p b h r -> p (b h) r")
            need(e, e_lb, s)
            e_mx.by(e.tensor_reduce(mx[:, :], l3, AX.X, ALU.max))
            need(e, e_mx, s)
            e_sub.by(e.tensor_tensor(l3, l3, mx[:, :, None].broadcast_to([P, NB * H, 3]), ALU.subtract))
            need(e, e_ex, s)
            e_sm.by(e.tensor_reduce(sm[:, :], l3, AX.X, ALU.add))
            need(e, e_sm, s)
            e_rs.by(e.reciprocal(rs[:, :], sm[:, :]))
            need(e, e_rs, s)
            need(e, e_m0, s - 1)
            need(e, e_m1, s - 1)
            need(e, e_m2, s - 1)
            e_gw.by(e.tensor_tensor(w3, l3, rs[:, :, None].broadcast_to([P, NB * H, 3]), ALU.mult))
        sk.add("dve", 1, f)

        def f(e, s):
            need(e, e_sub, s)
            e_ex.by(e.activation(lg[:, :, :, :], lg[:, :, :, :], ACT.Exp))
        sk.add("act", 1, f)

        sk.window(0.95, 1.0)
        for b in range(NB):
            def f(e, s, b=b):
                need(e, e_gw, s)
                need(e, e_ft, s, 3 * b + 2)
                need(e, e_Xy, s, b)
                e_m2.by(e.tensor_tensor(hv(y, b), hv(vtok, b), wide(gw[:, b, :, 2]), ALU.mult))
                e_m0.by(e.tensor_tensor(hv(ms, b), hv(ms, b), wide(gw[:, b, :, 0]), ALU.mult))
            sk.add("pool", 1, f)

            def f(e, s, b=b):
                need(e, e_gw, s)
                need(e, e_ft, s, 3 * b + 2)
                e_m1.by(e.tensor_tensor(hv(dl, b), hv(dl, b), wide(gw[:, b, :, 1]), ALU.mult))
                need(e, e_m1, s, b)
                need(e, e_m0, s, b)
                need(e, e_m2, s, b)
                e_a1.by(e.tensor_tensor(dl[:, b, :], dl[:, b, :], ms[:, b, :], ALU.add))
                need(e, e_a1, s, b)
                e_a2.by(e.tensor_tensor(dl[:, b, :], dl[:, b, :], y[:, b, :], ALU.add))
            sk.add("dve", 1, f)

            def f(e, s, b=b):
                need(e, e_a2, s, b)
                need(e, e_so, s, 0) if b else need(e, e_so, s - 1, 1)
                e_sqo.by(e.activation(rl[:, :], dl[:, b, :], ACT.Square))
            sk.add("act", 1, f)

            def f(e, s, b=b):
                need(e, e_sqo, s, b)
                need(e, e_ro, s - 1, b)
                e_so.by(e.tensor_reduce(so[:, b, :], rl[:, :].rearrange("p (h d) -> p h d", h=H), AX.X, ALU.add))
            sk.add("dve", 1, f)

            def f(e, s, b=b):
                need(e, e_so, s, b)
                need(e, e_rro, s - 1, b)
                e_ro.by(e.activation(ro[:, b, :], so[:, b, :], ACT.Sqrt, bias=eps[:, 2:3], scale=1.0 / P))
            sk.add("act", 1, f)

            def f(e, s, b=b):
                need(e, e_ro, s, b)
                e_rro.by(e.reciprocal(rro[:, b, :], ro[:, b, :]))
                need(e, e_rro, s, b)
                need(e, e_a2, s, b)
                e_on.by(e.tensor_tensor(hv(dl, b), hv(dl, b), wide(rro[:, b, :]), ALU.mult))
            sk.add("dve", 1, f)

            def f(e, s, b=b):
                need(e, e_on, s, b)
                need(e, e_oT, s, 0) if b else need(e, e_X, s)
                for h in range(H):
                    i = e.transpose(turn[:, hs(h)], dl[:, b, hs(h)], ident)
                e_oTp.by(i)
            sk.add("pe", 1, f)

            def f(e, s, b=b):
                need(e, e_oTp, s, b)
                need(e, e_cm, s)
                e_oT.by(e.copy(ym[:, :, hs(b)], bh(turn)))
            sk.add("act", 1, f)

            def f(e, s, b=b):
                need(e, e_oT, s, b)
                need(e, e_h, s, HB // 2 - 2 + b)
                for h in range(H):
                    i = e.matmul(dense[b][:, :], ym[:, h, hs(b)], wo[:, h, :], start=(h == 0), stop=(h == H - 1))
                e_att.by(i)
            sk.add("pe", 1, f)

            def f(e, s, b=b):
                need(e, e_att, s, b)
                need(e, e_res, s, b)
                e_xb.by(e.tensor_tensor(xb[:, b, :], xb[:, b, :], dense[b][:, :], ALU.add))
            sk.add("dve", 1, f)

        def f(e, s):
            need(e, e_xb, s)
            e.dma_start(out[:, bass.ds(s * P, P), :].rearrange("b p d -> p b d"), xb[:, :, :]).then_inc(stored, 16)
        sk.add("sp", 1, f)
        sk.flush()

        loads = [
            (wq[:, :, :], w["wq"].rearrange("(k p) n -> p k n", p=P)),
            (wk[:, :, :], w["wk"].rearrange("(k p) n -> p k n", p=P)),
            (wv[:, :, :], w["wv"].rearrange("(k p) n -> p k n", p=P)),
            (wr[:, :, :], w["wrT"].rearrange("(k p) n -> p k n", p=P)),
            (wfk[:, :, :], w["wfkT"].rearrange("(k p) n -> p k n", p=P)),
            (wfv[:, :, :], w["wfvT"].rearrange("(k p) n -> p k n", p=P)),
            (cm[:, :, :], w["cm"].rearrange("(k p) n -> p k n", p=P)),
            (wo[:, :, :], w["wo"].rearrange("(k p) n -> p k n", p=P)),
            (w1[:, :, :], w["w1"][0:D, :].rearrange("(k p) n -> p k n", p=P)),
            (w1x[:, :], w["w1"][D:D + NF, :]),
            (km[:, :, :], w["km"].rearrange("(k p) n -> p k n", p=P)),
            (w2[:, :, :], w["w2"].rearrange("(k p) n -> p k n", p=P)),
            (b1[:, :], w["b1"]),
            (b2[:, :], w["b2"][None, :].broadcast_to([P, NF])),
            (wb[:, :, :], w["wb"].rearrange("(k p) n -> p k n", p=P)),
            (onw[:, :], w["onw"].rearrange("(p a) -> p a", a=1)),
            (mu[:, 0, :], w["mu_r"]),
            (mu[:, 1, :], w["mu_k"]),
            (cst[:, :], w["cst"]),
        ]
        for j, n in enumerate(("cq", "ck", "cv")):
            loads.append((cw[:, j, :, :], w[n].rearrange("(c p) k -> p c k", p=P)))
        for j, t in enumerate(TAPS):
            loads.append((mw[:, WOFF[j]:WOFF[j] + CB * t].rearrange("p (c k) -> p c k", k=t),
                          w[f"m{t}"].rearrange("(c p) k -> p c k", p=P)))
        NLOAD = 16 * len(loads)
        NSET = 7

        def start_load(e):
            for dst, src in loads:
                e.dma_start(dst, src).then_inc(wload, 16)

        def start_pool(e):
            for t in (S[:, :, :], halo[:, :, :, :], vT[:, :, :, :], xsh[:, :, :, :]):
                e.memset(t, 0.0).then_inc(setup, 1)
            for i, v in enumerate((1e-5, 1e-6, 1e-5)):
                e.memset(eps[:, i:i + 1], v).then_inc(setup, 1)

        def start_dve(e):
            for k in range(CB):
                e.tensor_scalar(wo[:, k, :], wo[:, k, :], onw[:, 0:1], None, ALU.mult).then_inc(wol, 1)

        def both(k):
            return sorted([(p, 0, fn) for p, fn in sk.order(k)] + [(p, 1, fn) for p, fn in sf.order(k)],
                          key=lambda t: t[:2])

        def program(e, k):
            e.wait_ge(setup, NSET)
            if k != "sp":
                e.wait_ge(wload, NLOAD)
            if k == "dve":
                start_dve(e)
            if k == "pe":
                e.wait_ge(wol, CB)
            for _, fn in sf.order(k):
                fn(e, 0)
            for _, is_front, fn in both(k):
                fn(e, 1 if is_front else 0)
            with e.Fori(2, NS) as s:
                for _, is_front, fn in both(k):
                    fn(e, s if is_front else s - 1)
            for _, fn in sk.order(k):
                fn(e, NS - 1)
            if k == "sp":
                e.wait_ge(stored, 16 * NS)

        block = ctx.enter_context(nc.Block())

        @block.sync
        def _(e):
            start_load(e)
            program(e, "sp")

        @block.gpsimd
        def _(e):
            start_pool(e)
            program(e, "pool")

        @block.vector
        def _(e):
            program(e, "dve")

        @block.scalar
        def _(e):
            program(e, "act")

        @block.tensor
        def _(e):
            program(e, "pe")

        for name, ev in events:
            assert ev.seen == 3 * ev.n, (name, ev.seen, ev.n)


def kernel(**inputs):
    import numpy as np
    import concourse.bacc as bacc
    from concourse.bass_utils import run_bass_kernel_spmd

    n = len(LEVELS)
    cst = np.zeros((P, (n + 3) * P + 2), np.float32)
    r, c = np.arange(P)[:, None], np.arange(P)[None, :]
    for i, b in enumerate(LEVELS):
        cst[:, i * P:(i + 1) * P] = (r // (2 * b) == c // (2 * b)) & (r // b % 2 == 1) & (c // b % 2 == 0)
    cst[:, C_UP * P:(C_UP + 1) * P] = r < c
    cst[:, C_UPI * P:(C_UPI + 1) * P] = r <= c
    cst[:, C_ID * P:(C_ID + 1) * P] = r == c
    cst[:, C_ONE:] = 1.0

    a = {k: np.asarray(v) for k, v in inputs.items()}
    A = "L0_attn_"
    arrays = {
        "x": a[A + "hidden_states"], "wq": a[A + "Wq"], "wk": a[A + "Wk"], "wv": a[A + "Wv"], "wb": a[A + "Wb"],
        "cq": a[A + "conv_q_w"], "ck": a[A + "conv_k_w"], "cv": a[A + "conv_v_w"],
        "m3": a[A + "ms_w3"], "m15": a[A + "ms_w15"], "m31": a[A + "ms_w31"],
        "km": a[A + "kernel_mix_w"], "cm": a[A + "channel_mixer_w"],
        "w1": a[A + "fusion_w1"], "b1": a[A + "fusion_b1"].reshape(HB, P).T, "w2": a[A + "fusion_w2"], "b2": a[A + "fusion_b2"],
        "onw": a[A + "o_norm_w"], "wo": a[A + "Wo"],
        "wrT": a["L0_ffn_W_r"].T, "wfkT": a["L0_ffn_W_k"].T, "wfvT": a["L0_ffn_W_v"].T,
        "mu_r": a["L0_ffn_mu_r"].reshape(CB, P).T, "mu_k": a["L0_ffn_mu_k"].reshape(CB, P).T, "cst": cst,
    }
    arrays = {k: np.ascontiguousarray(v) for k, v in arrays.items()}
    nc = bacc.Bacc("TRN2", target_bir_lowering=False, num_devices=1)
    arrays = {f"in_{k}": v for k, v in arrays.items()}
    aps = {k[3:]: nc.dram_tensor(k, v.shape, F32, kind="ExternalInput").ap() for k, v in arrays.items()}
    out = nc.dram_tensor("out", arrays["in_x"].shape, F32, kind="ExternalOutput").ap()
    x = aps.pop("x")
    build(nc, x, out, aps)
    r = run_bass_kernel_spmd(nc, [arrays], core_ids=[0])
    return r.results[0]["out"]
```

```python
from contextlib import ExitStack

import concourse.bass as bass
from concourse import mybir

F32 = mybir.dt.float32
ALU = mybir.AluOpType
ACT = mybir.ActivationFunctionType
AX = mybir.AxisListType

P = 128
H = 4
D = H * P
NB = 2
W = NB * P
CB = D // P
HID = 2 * D
HB = HID // P
TAPS = (3, 15, 31)
SK = 4
SH = SK - 1
VH = max(TAPS) - 1
NF = 3 * H
LEVELS = [1 << i for i in range(7)]
WOFF = [0, TAPS[0] * CB, (TAPS[0] + TAPS[1]) * CB]
HP = P // 2
C_UP, C_UPI, C_ID = range(3)
C_LEV = 3 * P
C_ONE = C_LEV + len(LEVELS) * HP


class Event:

    def __init__(self, sem, n):
        self.sem, self.n, self.seen = sem, n, 0

    def at(self, s, i):
        return s * self.n + i + 1

    def by(self, ins):
        self.seen += 1
        ins.then_inc(self.sem, 1)


def need(e, ev, s, i=None):
    if isinstance(s, int) and s < 0:
        return
    e.wait_ge(ev.sem, ev.at(s, ev.n - 1 if i is None else i))


class Chain:

    def __init__(self, sem):
        self.sem, self.n = sem, 0

    def restart(self, e, first):
        if not first:
            e.wait_ge(self.sem, self.n)
            e.sem_clear(self.sem)
        self.n = 0

    def link(self, ins):
        self.n += 1
        ins.then_inc(self.sem, 1)
        return self.n

    def after(self, e, n):
        e.wait_ge(self.sem, n)


class Schedule:

    def __init__(self):
        self.items = []
        self.group = []

    def window(self, a, b):
        self.flush()
        self.a, self.b = a, b

    def add(self, eng, cost, fn, lag=0.0):
        self.group.append((eng, cost, fn, lag))

    def flush(self):
        total, t = sum(c for _, c, _, _ in self.group), 0.0
        for eng, c, fn, lag in self.group:
            self.items.append((self.a + (self.b - self.a) * t / total + lag, eng, fn, c))
            t += c
        self.group = []

    def order(self, eng):
        return sorted(((p, fn) for p, k, fn, _ in self.items if k == eng), key=lambda t: t[0])

    def fill(self, eng, cost, fns, others, a, b):
        bins = 200
        load = [0.0] * bins
        for o in others:
            for p, k, _, c in o.items:
                if k == eng:
                    load[min(int(p * bins), bins - 1)] += c
        window = range(int(a * bins), int(b * bins))
        level, room = 0.0, []
        while sum(room) < cost * len(fns):
            level += 0.01
            room = [max(0.0, level - sum(load[i - 4:i + 5] if i >= 4 else load[:i + 5]) / 9) for i in window]
        t, i = 0.0, 0
        for n, fn in enumerate(fns):
            while t < (n + 0.5) * cost and i < len(room) - 1:
                t, i = t + room[i], i + 1
            self.items.append(((window[0] + i) / bins, eng, fn, cost))


def build(nc, x, out, w):
    NS = x.shape[1] // P
    with ExitStack() as ctx:
        def sb(name, *shape):
            return ctx.enter_context(nc.sbuf_tensor(name, list(shape), F32))

        def bank(name):
            return ctx.enter_context(nc.psum_tensor(name, [P, 512], F32))

        def event(name, n):
            ev = Event(ctx.enter_context(nc.semaphore(name)), n)
            events.append((name, ev))
            return ev

        events = []

        wq, wk, wv = (sb(n, P, CB, D) for n in ("wq", "wk", "wv"))
        wr, wfk, wfv = (sb(n, P, CB, D) for n in ("wr", "wfk", "wfv"))
        cm, wo = sb("cm", P, CB, D), sb("wo", P, CB, D)
        w1 = sb("w1", P, CB, HID)
        w1x = sb("w1x", NF, HID)
        km = sb("km", P, 3, P)
        w2 = sb("w2", P, HB, NF)
        b1 = sb("b1", P, HB)
        b2 = sb("b2", P, NF)
        wb = sb("wb", P, CB, H)
        onw = sb("onw", P, 1)
        mu = sb("mu", P, 2, CB)
        cw = sb("cw", P, 3, CB, SK)
        mw = sb("mw", P, sum(TAPS) * CB)
        cst = sb("cst", P, C_ONE + 2)
        eps = sb("eps", P, 3)
        ident = cst[:, C_ID * P:(C_ID + 1) * P]
        ones = cst[:, C_ONE:C_ONE + 1]

        def mask(i):
            return cst[:, i * P:(i + 1) * P][:, None, :].broadcast_to([P, H, P])

        def level_mask(l):
            k = LEVELS[l]
            m = cst[:, C_LEV + l * HP:C_LEV + (l + 1) * HP].rearrange("p (n k) -> p n k", k=k)
            return m[:, None, :, :].broadcast_to([P, H, HP // k, k])

        def even(t, k):
            return t.rearrange("p (n k) -> p n k", k=2 * k)[:, :, 0:k]

        xa = sb("xa", P, NB, D)
        xb = sb("xb", P, NB, D)
        xnT = sb("xnT", P, CB, W)
        xsh = sb("xsh", P, CB, NB, 1 + P)
        xr, xk = sb("xr", P, CB, W), sb("xk", P, CB, W)
        rl = sb("rl", P, 2 * W)
        ka = sb("ka", P, CB, W)
        th = sb("th", P, D)
        raw = [sb(f"raw{i}", P, 2, NB, SH + P) for i in range(2)]
        halo = sb("halo", P, 3 * CB, NB, SH)
        qT, kT = sb("qT", P, CB, W), sb("kT", P, CB, W)
        vT = sb("vT", P, CB, NB, VH + P)
        ktok, vtok = sb("ktok", P, NB, D), sb("vtok", P, NB, D)
        y, u = sb("y", P, NB, D), sb("u", P, NB, D)
        Bm, Y, X, aT = (sb(n, P, NB, D) for n in ("Bm", "Y", "X", "aT"))
        Wm = sb("Wm", P, NB, H * HP)
        S = sb("S", P, NB, D)
        dl = sb("dl", P, NB, D)
        my = [sb(f"my{i}", P, 3, W) for i in range(2)]
        ym = sb("ym", P, CB, W)
        ms = sb("ms", P, NB, D)
        bst, mv = sb("bst", P, NB, 6), sb("mv", P, NB, 2)
        std, rstd, nmr = sb("std", P, NB), sb("rstd", P, NB), sb("nmr", P, NB)
        nrm, rn = sb("nrm", P, NB, 2 * H), sb("rn", P, NB, 2 * H)
        bt, gt, g = sb("bt", P, NB, H), sb("gt", P, NB, H), sb("g", P, NB, H)
        ft, ftT = sb("ft", P, NB, NF), sb("ftT", NF, W)
        lg, gw = sb("lg", P, NB, H, 3), sb("gw", P, NB, H, 3)
        mx, sm, rs = sb("mx", P, NB * H), sb("sm", P, NB * H), sb("rs", P, NB * H)
        so, ro, rro = sb("so", P, NB, H), sb("ro", P, NB, H), sb("rro", P, NB, H)
        oT = sb("oT", P, CB, W)
        sq = u[:, :, :].rearrange("p b (c w) -> p (b c) w", w=W)
        hd = [t[:, c, :] for t in (xr, xk) for c in range(CB)]

        front = [bank(f"front{i}") for i in range(2)]
        dense = [bank(f"dense{i}") for i in range(2)]
        cell = [bank(f"cell{b}") for b in range(NB)]
        turn = bank("turn")
        small = bank("small")
        s_norm = front[0][:, 0:NB * 2 * H]
        s_beta = front[0][:, 32:32 + NB * H]
        s_ft = small[0:NF, 64:64 + W]
        s_mix = small[:, 64:64 + W]
        s_lg = small[:, 384:384 + NB * NF]

        def hv(t, b):
            return t[:, b, :].rearrange("p (h d) -> p h d", h=H)

        def bh(t):
            return t[:, :].rearrange("p (h d) -> p h d", h=H)

        def wide(col):
            return col[:, :, None].broadcast_to([P, H, P])

        def hs(h):
            return slice(h * P, (h + 1) * P)

        held = ctx.enter_context(nc.semaphore("held"))

        def hold(e):
            e.sem_inc(held, 1)

        chain = Chain(ctx.enter_context(nc.semaphore("dve_chain")))
        wload = ctx.enter_context(nc.semaphore("wload"))
        setup = ctx.enter_context(nc.semaphore("setup"))
        wol = ctx.enter_context(nc.semaphore("wo_scaled"))
        xa_in = ctx.enter_context(nc.semaphore("xa_in"))
        xb_in = ctx.enter_context(nc.semaphore("xb_in"))
        stored = ctx.enter_context(nc.semaphore("stored"))

        sf, sk, sc = Schedule(), Schedule(), Schedule()

        e_stat, e_agg = event("e_stat", NB), event("e_agg", NB)
        e_std, e_rstd, e_nmr = event("e_std", 1), event("e_rstd", 1), event("e_nmr", 1)
        e_xn, e_xT, e_xnT = event("e_xn", NB), event("e_xT", NB), event("e_xnT", NB)
        e_proj, e_raw = event("e_proj", 6), event("e_raw", 6)
        e_hin, e_hout = event("e_hin", 6), event("e_hout", 6)
        e_vh = event("e_vh", 1)
        e_cv = event("e_cv", 6 * 2)
        e_act = event("e_act", 6)
        e_xcp = event("e_xcp", 2)
        e_msc = event("e_msc", 3 * H)
        e_tk, e_sqk = event("e_tk", 2 * NB), event("e_sq", 2)
        e_S, e_KTu = event("e_S", NB), event("e_KTu", NB)
        e_o = event("e_o", NB)
        e_xb = event("e_xb", NB)
        e_gr, e_qk = event("e_gr", NB), event("e_qk", NB)

        e_fmm, e_frl, e_ka = event("e_fmm", 2), event("e_frl", 2), event("e_ka", 2)
        e_dx, e_xrk = event("e_dx", 1), event("e_xrk", 2 * CB)
        e_r, e_th = event("e_r", NB), event("e_th", NB)
        e_kv, e_gate = event("e_kv", NB), event("e_gate", NB)
        e_res = event("e_res", NB)
        e_nn, e_bm = event("e_nn", 2), event("e_bm", 1)
        e_nrm, e_rn, e_bt, e_b2, e_gt, e_g = (event(n, 1) for n in ("e_nrm", "e_rn", "e_bt", "e_b2", "e_gt", "e_g"))
        e_tT = event("e_tT", 2 * NB)
        e_vn = event("e_vn", NB)
        e_B, e_aT = event("e_B", NB * H), event("e_aT", NB)
        e_Yo = event("e_Yo", NB)
        NL = len(LEVELS)
        e_Wp, e_W = event("e_Wp", NB * NL), event("e_W", NB * NL)
        e_Xp, e_X = event("e_Xp", NB * NL), event("e_X", NB * NL)
        e_Zp, e_Y = event("e_Zp", NB * (NL - 1)), event("e_Y", NB * NL)
        e_KS, e_y, e_Xy, e_u = (event(n, NB) for n in ("e_KS", "e_y", "e_Xy", "e_u"))
        e_d = event("e_d", NB)
        e_km, e_ym = event("e_km", H), event("e_ym", H)
        e_cm, e_ms = event("e_cm", NB), event("e_ms", NB)
        e_ft = event("e_ft", 3 * NB)
        e_fp, e_fT = event("e_fp", NB), event("e_fT", NB)
        e_z, e_h, e_l = event("e_z", HB // 2), event("e_h", HB // 2), event("e_l", HB // 2)
        e_lb, e_mx, e_sub, e_ex, e_sm, e_rs, e_gw = (
            event(n, 1) for n in ("e_lb", "e_mx", "e_sub", "e_ex", "e_sm", "e_rs", "e_gw"))
        e_m0, e_m1, e_m2 = event("e_m0", NB), event("e_m1", NB), event("e_m2", NB)
        e_a1, e_a2 = event("e_a1", NB), event("e_a2", NB)
        e_sqo, e_so, e_ro, e_rro, e_on = (event(n, NB) for n in ("e_sqo", "e_so", "e_ro", "e_rro", "e_on"))
        e_oTp, e_oT, e_att = event("e_oTp", NB), event("e_oT", NB), event("e_att", NB)

        sf.window(0.0, 0.05)

        def f(e, s):
            need(e, e_xT, s - 1)
            e.dma_start(xa[:, :, :], x[:, bass.ds(s * P, P), :].rearrange("b p d -> p b d")).then_inc(xa_in, 16)
        sf.add("sp", 1, f)

        sf.window(0.22, 0.24)

        def f(e, s):
            e.wait_ge(xa_in, s * 16 + 16)
            for b in range(NB):
                e_stat.by(e.bn_stats(bst[:, b, :], xa[:, b, :]))
            for b in range(NB):
                need(e, e_stat, s, b)
                if b == 0:
                    need(e, e_xn, s - 1)
                hold(e)
                e_agg.by(e.bn_aggr(mv[:, b, :], bst[:, b, :]))
        sf.add("dve", 2, f)

        def f(e, s):
            need(e, e_agg, s)
            need(e, e_rstd, s - 1)
            e_std.by(e.activation(std[:, :], mv[:, :, 1], ACT.Sqrt, bias=eps[:, 0:1]))
        sf.add("act", 1, f)

        def f(e, s):
            need(e, e_std, s)
            e_rstd.by(e.reciprocal(rstd[:, :], std[:, :]))
            need(e, e_rstd, s)
            e_nmr.by(e.scalar_tensor_tensor(nmr[:, :], mv[:, :, 0], -1.0, rstd[:, :], ALU.mult, ALU.mult))
        sf.add("dve", 1, f)

        sf.window(0.30, 0.36)
        for b in range(NB):
            def f(e, s, b=b):
                e.wait_ge(xa_in, s * 16 + 16)
                need(e, e_nmr, s)
                e_xn.by(e.activation(xa[:, b, :], xa[:, b, :], ACT.Identity, bias=nmr[:, b:b + 1],
                                     scale=rstd[:, b:b + 1]))
            sf.add("act", 1, f)

            def f(e, s, b=b):
                need(e, e_xn, s, b)
                if b == 0:
                    need(e, e_bt, s - 1)
                    need(e, e_nrm, s - 1)
                else:
                    need(e, e_raw, s - 1, 5)
                for c in range(CB):
                    i = e.transpose(front[b][:, hs(c)], xa[:, b, hs(c)], ident)
                e_xT.by(i)
            sf.add("pe", 1, f)

            def f(e, s, b=b):
                need(e, e_xT, s, b)
                need(e, e_xcp, s - 1)
                need(e, e_bm, s - 1)
                e_xnT.by(e.copy(xnT[:, :, hs(b)], bh(front[b])))
            sf.add("act", 1, f)

        PROJ_AT = ((0.60, 0.66), (0.72, 0.77), (0.84, 0.87))
        CONV_LAG = (0.09, 0.04, 0.07)
        for pair in range(6):
            j, c0 = pair // 2, 2 * (pair % 2)
            wt, r = (wq, wk, wv)[j], raw[pair % 2]
            if pair % 2 == 0:
                sf.window(*PROJ_AT[j])

            def f(e, s, pair=pair, wt=wt, c0=c0):
                if pair == 0:
                    need(e, e_xnT, s)
                if pair < 2:
                    need(e, e_xnT, s, pair)
                else:
                    need(e, e_raw, s, pair - 2)
                for c in range(2):
                    for k in range(CB):
                        i = e.matmul(front[pair % 2][:, c * W:(c + 1) * W], wt[:, k, hs(c0 + c)], xnT[:, k, :],
                                     start=(k == 0), stop=(k == CB - 1))
                e_proj.by(i)
            sf.add("pe", 2, f)

            def f(e, s, pair=pair, r=r):
                need(e, e_cv, s if pair >= 2 else s - 1, 2 * ((pair - 2) % 6) + 1)
                if pair == 4:
                    need(e, e_msc, s - 1)
                    need(e, e_tk, s - 1)
                    hold(e)
                    e_vh.by(e.tensor_copy(vT[:, :, :, 0:VH], vT[:, :, :, P:P + VH]))
                need(e, e_hout, s - 1, pair)
                hold(e)
                e_hin.by(e.tensor_copy(r[:, :, :, 0:SH],
                                       halo[:, 2 * pair:2 * pair + 2, :, :]))
            sf.add("pool", 1, f)

            def f(e, s, pair=pair, r=r):
                need(e, e_proj, s, pair)
                if pair >= 2:
                    need(e, e_cv, s, 2 * (pair - 2) + 1)
                    need(e, e_hout, s, pair - 2)
                else:
                    need(e, e_cv, s - 1, 2 * (pair + 4) + 1)
                    need(e, e_hout, s - 1, pair + 4)
                for c in range(2):
                    i = e.copy(r[:, c, :, SH:SH + P],
                               front[pair % 2][:, c * W:(c + 1) * W].rearrange("p (b t) -> p b t", b=NB))
                e_raw.by(i)
            sf.add("act", 1, f)

            def f(e, s, pair=pair, r=r):
                need(e, e_raw, s, pair)
                need(e, e_hin, s, pair)
                hold(e)
                e_hout.by(e.tensor_copy(halo[:, 2 * pair:2 * pair + 2, :, :], r[:, :, :, P:P + SH]))
            sf.add("pool", 1, f)

            def dst(c, j=j, c0=c0):
                if j == 2:
                    return vT[:, c0 + c, :, VH:VH + P]
                return (qT, kT)[j][:, c0 + c, :].rearrange("p (b t) -> p b t", b=NB)

            def f(e, s, pair=pair, r=r, j=j, c0=c0, dst=dst):
                need(e, e_raw, s, pair)
                need(e, e_hin, s, pair)
                if pair == 0:
                    need(e, e_o, s - 1)
                    need(e, e_qk, s - 1)
                    need(e, e_nn, s - 1)
                if pair == 2:
                    need(e, e_KTu, s - 1)
                    need(e, e_tk, s - 1)
                if pair == 4:
                    need(e, e_vh, s)
                last = {}
                for t in range(SK):
                    for c in range(2):
                        src, wc = r[:, c, :, t:t + P], cw[:, j, c0 + c, t:t + 1]
                        if t == 0:
                            i = e.tensor_scalar(dst(c), src, wc, None, ALU.mult)
                        else:
                            chain.after(e, last[c])
                            i = e.scalar_tensor_tensor(dst(c), src, wc, dst(c), ALU.mult, ALU.add)
                        if t < SK - 1:
                            last[c] = chain.link(i)
                        else:
                            e_cv.by(i)
            sf.add("dve", 5, f, CONV_LAG[j])

            def f(e, s, pair=pair, dst=dst):
                need(e, e_cv, s, 2 * pair + 1)
                for c in range(2):
                    i = e.activation(dst(c), dst(c), ACT.Silu)
                e_act.by(i)
            sf.add("act", 2, f, CONV_LAG[j] + 0.02)
        sf.window(0.90, 0.96)

        def f(e, s):
            need(e, e_act, s, 1)
            need(e, e_KTu, s - 1)
            e_sqk.by(e.activation(sq, qT[:, :, :], ACT.Square))
            need(e, e_act, s, 3)
            need(e, e_nn, s, 0)
            e_sqk.by(e.activation(sq, kT[:, :, :], ACT.Square))
        sf.add("act", 1, f)

        def f(e, s):
            need(e, e_raw, s, 4)
            for b in range(NB):
                for k in range(CB):
                    i = e.matmul(s_beta[:, b * H:(b + 1) * H], xnT[:, k, hs(b)], wb[:, k, :],
                                 start=(k == 0), stop=(k == CB - 1))
            e_bm.by(i)
            for j in range(2):
                need(e, e_sqk, s, j)
                for b in range(NB):
                    for h in range(H):
                        n = b * 2 * H + j * H + h
                        i = e.matmul(s_norm[:, n:n + 1], sq[:, h, hs(b)], ones, start=True, stop=True)
                e_nn.by(i)
        sf.add("pe", 1, f)

        def f(e, s):
            need(e, e_bm, s)
            need(e, e_nn, s)
            need(e, e_b2, s - 1)
            e_bt.by(e.activation(bt[:, :, :], s_beta.rearrange("p (b n) -> p b n", b=NB), ACT.Tanh, scale=0.5))
            need(e, e_d, s - 1)
            need(e, e_vn, s - 1)
            e_nrm.by(e.activation(nrm[:, :, :], s_norm.rearrange("p (b n) -> p b n", b=NB), ACT.Sqrt,
                                  bias=eps[:, 1:2]))
        sf.add("act", 1, f)

        def f(e, s):
            need(e, e_bt, s)
            e_b2.by(e.tensor_scalar(gt[:, :, :], bt[:, :, :], 0.5, 0.5, ALU.mult, ALU.add))
            need(e, e_nrm, s)
            e_rn.by(e.reciprocal(rn[:, :, :], nrm[:, :, :]))
            need(e, e_rn, s)
            need(e, e_b2, s)
            e_gt.by(e.tensor_tensor(gt[:, :, :], gt[:, :, :], rn[:, :, H:2 * H], ALU.mult))
            need(e, e_gt, s)
            need(e, e_B, s - 1)
            need(e, e_u, s - 1)
            e_g.by(e.tensor_tensor(g[:, :, :], gt[:, :, :], rn[:, :, H:2 * H], ALU.mult))
        sf.add("dve", 1, f)
        sf.flush()

        sk.window(0.50, 0.51)

        def f(e, s):
            if not (isinstance(s, int) and s == 0):
                e.wait_ge(stored, s * 16)
            e.dma_start(xb[:, :, :], x[:, bass.ds(s * P, P), :].rearrange("b p d -> p b d")).then_inc(xb_in, 16)
        sk.add("sp", 1, f)

        sk.window(0.29, 0.30)

        def f(e, s):
            need(e, e_xnT, s)
            need(e, e_z, s - 1)
            need(e, e_xrk, s - 1)
            hold(e)
            e_xcp.by(e.tensor_copy(xsh[:, :, :, 0:1], xsh[:, :, :, P:P + 1]))
            need(e, e_xcp, s, 0)
            hold(e)
            e_xcp.by(e.tensor_copy(xsh[:, :, :, 1:1 + P], xnT[:, :, :].rearrange("p c (b t) -> p c b t", b=NB)))
        sk.add("pool", 1, f)

        def token_major(b, j):
            tok, n = (ktok, vtok)[j], NB * j + b

            def f(e, s):
                need(e, e_act, s, 3 + 2 * j)
                if n == 0:
                    need(e, e_X, s - 1)
                elif n == NB:
                    need(e, e_X, s, NB * (NL - 1) - 1)
                else:
                    need(e, e_tk, s, n - 1)
                for h in range(H):
                    t = kT[:, h, hs(b)] if j == 0 else vT[:, h, b, VH:VH + P]
                    i = e.transpose(turn[:, hs(h)], t, ident)
                e_tT.by(i)
            sk.add("pe", 1, f)

            def f(e, s):
                need(e, e_tT, s, n)
                need(e, (e_KTu, e_m2)[j], s - 1, b)
                if j:
                    need(e, e_ft, s - 1, 3 * b + 2)
                e_tk.by(e.copy(tok[:, b, :], turn[:, :]))
            sk.add("act", 1, f)

        sk.window(0.0, 0.08)
        for b in range(NB):
            token_major(b, 0)

            def f(e, s, b=b):
                if b == 0:
                    need(e, e_act, s, 3)
                need(e, e_S, s - 1, b)
                for h in range(H):
                    i = e.matmul(cell[b][:, hs(h)], kT[:, h, hs(b)], kT[:, h, hs(b)], start=True, stop=True)
                e_gr.by(i)
            sk.add("pe", 1, f)

            def f(e, s, b=b):
                need(e, e_gr, s, b)
                need(e, e_g, s)
                need(e, e_Wp, s - 1, NB * (NL - 1) + b)
                for h in range(H):
                    e_B.by(e.scalar_tensor_tensor(Bm[:, b, hs(h)], cell[b][:, hs(h)], g[:, b, h:h + 1],
                                                  cst[:, C_UP * P:(C_UP + 1) * P], ALU.mult, ALU.mult))
            sk.add("dve", 1, f)

        for b in range(NB):
            def f(e, s, b=b):
                need(e, e_B, s, H * (b + 1) - 1)
                for h in range(H):
                    i = e.matmul(cell[b][:, hs(h)], kT[:, h, hs(b)], qT[:, h, hs(b)], start=True, stop=True)
                e_qk.by(i)
            sk.add("pe", 1, f)

            def f(e, s, b=b):
                need(e, e_qk, s, b)
                need(e, e_o, s - 1, b)
                e_aT.by(e.tensor_tensor(hv(aT, b), bh(cell[b]), mask(C_UPI), ALU.mult))
            sk.add("dve", 1, f)

        sk.window(0.08, 0.48)
        for l in range(NL):
            for b in range(NB):
                n = NB * l + b

                def f(e, s, l=l, b=b, n=n):
                    if l == 0:
                        need(e, e_aT, s, b)
                        for h in range(H):
                            i = e.transpose(cell[b][:, hs(h)], Bm[:, b, hs(h)], ident)
                        e_Wp.by(i)
                        return
                    need(e, e_Y, s, n - NB)
                    k = LEVELS[l]
                    for h in range(H):
                        i = e.matmul(cell[b][:, h * HP:(h + 1) * HP].rearrange("p (n k) -> p n k", k=k),
                                     Bm[:, b, hs(h)], even(Y[:, b, hs(h)], k), start=True, stop=True)
                    e_Wp.by(i)
                    m = n - NB
                    if m == 0:
                        need(e, e_tk, s, NB - 1)
                    else:
                        need(e, e_X, s, m - 1)
                    for h in range(H):
                        i = e.transpose(turn[:, hs(h)], Y[:, b, hs(h)], ident)
                    e_Xp.by(i)
                sk.add("pe", 2, f)

                def f(e, s, l=l, b=b, n=n):
                    need(e, e_Wp, s, n)
                    k = LEVELS[l]
                    if l == 0:
                        need(e, e_Zp, s - 1, NB * (NL - 2) + b)
                        src = even(cell[b][:, :], 1).rearrange("p (h n) k -> p h n k", h=H)
                    else:
                        src = cell[b][:, 0:H * HP].rearrange("p (h n k) -> p h n k", h=H, k=k)
                    e_W.by(e.tensor_tensor(Wm[:, b, :].rearrange("p (h n k) -> p h n k", h=H, k=k), src,
                                           level_mask(l), ALU.mult))
                sk.add("dve", 1, f)

                if l:
                    def f(e, s, b=b, n=n):
                        need(e, e_Xp, s, n - NB)
                        if n - NB < NB:
                            need(e, e_Xy, s - 1, b)
                        else:
                            need(e, e_Zp, s, n - 2 * NB)
                        e_X.by(e.copy(X[:, b, :], turn[:, :]))
                    sk.add("act", 1, f)
            for b in range(NB):
                n = NB * l + b
                if l:
                    def f(e, s, b=b, n=n):
                        need(e, e_W, s, n)
                        need(e, e_X, s, n - NB)
                        for h in range(H):
                            i = e.matmul(cell[b][:, h * HP:(h + 1) * HP], X[:, b, hs(h)],
                                         Wm[:, b, h * HP:(h + 1) * HP], start=True, stop=True)
                        e_Zp.by(i)
                    sk.add("pe", 2, f)

                if l == 0:
                    def f(e, s, b=b):
                        if b == 0:
                            need(e, e_Xp, s - 1)
                        e_Yo.by(e.tensor_tensor(
                            hv(Y, b).rearrange("p h (n k) -> p h n k", k=2)[:, :, :, 1],
                            mask(C_ID).rearrange("p h (n k) -> p h n k", k=2)[:, :, :, 1],
                            mask(C_ID).rearrange("p h (n k) -> p h n k", k=2)[:, :, :, 1], ALU.mult))
                    sk.add("pool", 1, f)

                def f(e, s, l=l, b=b, n=n):
                    k = LEVELS[l]
                    yv = even(Y[:, b, :], k).rearrange("p (h n) k -> p h n k", h=H)
                    wv_ = Wm[:, b, :].rearrange("p (h n k) -> p h n k", h=H, k=k)
                    if l == 0:
                        need(e, e_W, s, n)
                        if b == 0:
                            need(e, e_Xp, s - 1)
                        idv = mask(C_ID).rearrange("p h (n k) -> p h n k", k=2)[:, :, :, 0:1]
                        need(e, e_Yo, s, b)
                        e_Y.by(e.tensor_tensor(yv, idv, wv_, ALU.subtract))
                    else:
                        need(e, e_Zp, s, n - NB)
                        e_Y.by(e.tensor_tensor(yv, yv, cell[b][:, 0:H * HP].rearrange(
                            "p (h n k) -> p h n k", h=H, k=k), ALU.subtract))
                sk.add("dve", 1, f)

        sk.window(0.48, 0.51)
        for b in range(NB):
            token_major(b, 1)

            def f(e, s, b=b):
                need(e, e_tk, s, NB + b)
                need(e, e_nrm, s)
                need(e, e_a2, s - 1, b)
                e_vn.by(e.tensor_tensor(hv(y, b), hv(vtok, b), wide(nrm[:, b, H:2 * H]), ALU.mult))
            sk.add("pool", 1, f)

        sk.window(0.51, 0.69)
        for b in range(NB):
            m = NB * (NL - 1) + b

            def f(e, s, b=b, m=m):
                need(e, e_Y, s, m)
                need(e, e_tk, s) if b == 0 else need(e, e_X, s, m - 1)
                for h in range(H):
                    i = e.transpose(turn[:, hs(h)], Y[:, b, hs(h)], ident)
                e_Xp.by(i)
                need(e, e_S, s - 1, b)
                for h in range(H):
                    i = e.matmul(cell[b][:, hs(h)], kT[:, h, hs(b)], S[:, b, hs(h)], start=True, stop=True)
                e_KS.by(i)
            sk.add("pe", 1, f)

            def f(e, s, b=b, m=m):
                need(e, e_Xp, s, m)
                need(e, e_Zp, s, m - NB)
                e_X.by(e.copy(X[:, b, :], turn[:, :]))
            sk.add("act", 1, f)

            def f(e, s, b=b):
                need(e, e_KS, s, b)
                need(e, e_vn, s, b)
                e_y.by(e.tensor_tensor(y[:, b, :], y[:, b, :], cell[b][:, :], ALU.subtract))
            sk.add("dve", 1, f)
        for b in range(NB):
            m = NB * (NL - 1) + b

            def f(e, s, b=b, m=m):
                need(e, e_y, s, b)
                need(e, e_X, s, m)
                for h in range(H):
                    i = e.matmul(cell[b][:, hs(h)], X[:, b, hs(h)], y[:, b, hs(h)], start=True, stop=True)
                e_Xy.by(i)
            sk.add("pe", 1, f)

            def f(e, s, b=b):
                need(e, e_Xy, s, b)
                need(e, e_KTu, s - 1, b)
                e_u.by(e.tensor_tensor(hv(u, b), bh(cell[b]), wide(g[:, b, :]), ALU.mult))
            sk.add("dve", 1, f)
        for b in range(NB):
            def f(e, s, b=b):
                need(e, e_u, s, b)
                need(e, e_aT, s, b)
                for h in range(H):
                    e.matmul(cell[b][:, hs(h)], qT[:, h, hs(b)], S[:, b, hs(h)], start=True, stop=False)
                    i = e.matmul(cell[b][:, hs(h)], aT[:, b, hs(h)], u[:, b, hs(h)], start=False, stop=True)
                e_o.by(i)
            sk.add("pe", 1, f)

            def f(e, s, b=b):
                need(e, e_o, s, b)
                need(e, e_rn, s)
                need(e, e_on, s - 1, b)
                e_d.by(e.tensor_tensor(hv(dl, b), bh(cell[b]), wide(rn[:, b, 0:H]), ALU.mult))
            sk.add("dve", 1, f)
        for b in range(NB):
            def f(e, s, b=b):
                need(e, e_d, s, b)
                for h in range(H):
                    i = e.matmul(cell[b][:, hs(h)], ktok[:, b, hs(h)], u[:, b, hs(h)], start=True, stop=True)
                e_KTu.by(i)
            sk.add("pe", 1, f)

            def f(e, s, b=b):
                need(e, e_KTu, s, b)
                e_S.by(e.tensor_tensor(S[:, b, :], S[:, b, :], cell[b][:, :], ALU.add))
            sk.add("dve", 1, f)

        sk.window(0.31, 0.36)

        def f(e, s):
            need(e, e_xcp, s)
            need(e, e_fmm, s - 1)
            need(e, e_r, s - 1)
            xrv = ka[:, :, :].rearrange("p c (b t) -> p c b t", b=NB)
            need(e, e_l, s - 1)
            need(e, e_kv, s - 1)
            e_dx.by(e.tensor_tensor(xrv, xsh[:, :, :, 1:1 + P], xsh[:, :, :, 0:P], ALU.subtract))
            need(e, e_dx, s)
            for j, dst in enumerate((xr, xk)):
                for c in range(CB):
                    e_xrk.by(e.scalar_tensor_tensor(
                        dst[:, c, :].rearrange("p (b t) -> p b t", b=NB), xrv[:, c, :, :],
                        mu[:, j, c:c + 1], xsh[:, c, :, 0:P], ALU.mult, ALU.add))
        sk.add("dve", 1, f)

        sk.window(0.49, 0.85)
        for pair in range(2):
            def f(e, s, pair=pair):
                need(e, e_xrk, s)
                need(e, e_xb, s - 1, pair)
                for c in range(2):
                    for k in range(CB):
                        i = e.matmul(dense[pair][:, c * W:(c + 1) * W], wfk[:, k, hs(2 * pair + c)], xk[:, k, :],
                                     start=(k == 0), stop=(k == CB - 1))
                e_fmm.by(i)
            sk.add("pe", 2, f)

            def f(e, s, pair=pair):
                need(e, e_fmm, s, pair)
                need(e, e_ka, s, 0) if pair else need(e, e_so, s - 1)
                e_frl.by(e.activation(rl[:, :], dense[pair][:, :], ACT.Relu))
            sk.add("act", 1, f)

            def f(e, s, pair=pair):
                need(e, e_frl, s, pair)
                need(e, e_xrk, s)
                e_ka.by(e.scalar_tensor_tensor(ka[:, 2 * pair:2 * pair + 2, :],
                                               rl[:, :].rearrange("p (c w) -> p c w", c=2), 0.5,
                                               rl[:, :].rearrange("p (c w) -> p c w", c=2), ALU.mult, ALU.mult))
            sk.add("dve", 1, f)
        for b in range(NB):
            def f(e, s, b=b):
                need(e, e_xrk, s)
                need(e, e_frl, s, 0) if b == 0 else need(e, e_gate, s, 0)
                for k in range(CB):
                    i = e.matmul(dense[0][:, :], xr[:, k, hs(b)], wr[:, k, :], start=(k == 0), stop=(k == CB - 1))
                e_r.by(i)
                need(e, e_ka, s)
                need(e, e_frl, s, 1) if b == 0 else need(e, e_gate, s, 0)
                for k in range(CB):
                    i = e.matmul(dense[1][:, :], ka[:, k, hs(b)], wfv[:, k, :], start=(k == 0), stop=(k == CB - 1))
                e_kv.by(i)
            sk.add("pe", 4, f)

            def f(e, s, b=b):
                need(e, e_r, s, b)
                need(e, e_res, s, 0) if b else need(e, e_res, s - 1, 1)
                e_th.by(e.activation(th[:, :], dense[0][:, :], ACT.Tanh, scale=0.5))
            sk.add("act", 1, f)

            def f(e, s, b=b):
                need(e, e_th, s, b)
                need(e, e_kv, s, b)
                e_gate.by(e.scalar_tensor_tensor(th[:, :], th[:, :], 1.0, dense[1][:, :], ALU.add, ALU.mult))
            sk.add("dve", 1, f)

            def f(e, s, b=b):
                need(e, e_gate, s, b)
                e.wait_ge(xb_in, s * 16 + 16)
                e_res.by(e.tensor_tensor(xb[:, b, :], xb[:, b, :], th[:, :], ALU.add))
            sk.add("pool", 1, f)

        convs = [[] for _ in range(H)]
        for h in range(H):
            blocks = [((3 * h + p) // CB, (3 * h + p) % CB) for p in range(3)]
            plan = sorted((t, p) for p in range(3) for t in range(TAPS[blocks[p][0]]))
            last = {}
            for t, p in plan:
                j, c = blocks[p]

                def f(e, s, h=h, t=t, p=p, j=j, c=c, last=last):
                    if h == t == p == 0:
                        need(e, e_act, s)
                    o = my[h % 2][:, p, :].rearrange("p (b t) -> p b t", b=NB)
                    off = VH - (TAPS[j] - 1) + t
                    src = vT[:, c, :, off:off + P]
                    col = WOFF[j] + c * TAPS[j] + t
                    if t == 0:
                        if p == 0:
                            need(e, e_km, s - 1 if h < 2 else s, (h + 2) % H)
                        i = e.tensor_scalar(o, src, mw[:, col:col + 1], None, ALU.mult)
                    else:
                        chain.after(e, last[p])
                        i = e.scalar_tensor_tensor(o, src, mw[:, col:col + 1], o, ALU.mult, ALU.add)
                    if t < TAPS[j] - 1:
                        last[p] = chain.link(i)
                    else:
                        e_msc.by(i)
                convs[h].append(f)

        sk.flush()
        MIX_AT = (0.28, 0.30, 0.56, 0.92)
        for h in range(H):
            sk.window(MIX_AT[h], MIX_AT[h] + 0.01)

            def f(e, s, h=h):
                need(e, e_msc, s, 3 * h + 2)
                if h:
                    need(e, e_ym, s, h - 1)
                else:
                    need(e, e_lb, s - 1)
                for p in range(3):
                    i = e.matmul(s_mix, km[:, p, :], my[h % 2][:, p, :], start=(p == 0), stop=(p == 2))
                e_km.by(i)
            sk.add("pe", 1, f)

            def f(e, s, h=h):
                need(e, e_km, s, h)
                if h == 0:
                    need(e, e_cm, s - 1)
                e_ym.by(e.copy(ym[:, h, :], s_mix))
            sk.add("act", 1, f)
        sk.flush()

        sc.window(0.0, 0.07)
        for b in range(NB):
            def f(e, s, b=b):
                need(e, e_ym, s)
                need(e, (e_th, e_gate)[b], s)
                for k in range(CB):
                    i = e.matmul(dense[b][:, :], ym[:, k, hs(b)], cm[:, k, :], start=(k == 0), stop=(k == CB - 1))
                e_cm.by(i)
            sc.add("pe", 1, f)

            def f(e, s, b=b):
                need(e, e_cm, s, b)
                need(e, e_a1, s - 1, b)
                e_ms.by(e.copy(ms[:, b, :], dense[b][:, :]))
            sc.add("act", 1, f)

            def f(e, s, b=b):
                need(e, e_fp, s - 1, b)
                for j, (t, ev, i) in enumerate(((ms, e_ms, b), (dl, e_d, b), (vtok, e_tk, NB + b))):
                    need(e, ev, s, i)
                    e_ft.by(e.tensor_reduce(ft[:, b, j * H:(j + 1) * H], hv(t, b), AX.X, ALU.add,
                                            apply_absolute_value=True))
            sc.add("dve", 1, f)

            def f(e, s, b=b):
                need(e, e_ft, s, 3 * b + 2)
                need(e, e_ym, s)
                e_fp.by(e.matmul(s_ft[:, hs(b)], ft[:, b, :], ident, start=True, stop=True))
            sc.add("pe", 1, f)

        def f(e, s):
            need(e, e_fp, s)
            need(e, e_z, s - 1)
            for b in range(NB):
                e_fT.by(e.activation(ftT[:, hs(b)], s_ft[:, hs(b)], ACT.Copy, scale=1.0 / P))
        sc.add("act", 1, f)

        sc.window(0.07, 0.27)
        for pair in range(HB // 2):
            def f(e, s, pair=pair):
                if pair < 2:
                    need(e, e_ms, s, pair)
                else:
                    need(e, e_h, s, pair - 2)
                need(e, e_fT, s)
                for c in range(2):
                    o = dense[pair % 2][:, c * W:(c + 1) * W]
                    for k in range(CB):
                        e.matmul(o.rearrange("p (b t) -> p b t", b=NB), w1[:, k, hs(2 * pair + c)],
                                 xsh[:, k, :, 1:1 + P], start=(k == 0), stop=False)
                    i = e.matmul(o, w1x[:, hs(2 * pair + c)], ftT[:, :], start=False, stop=True)
                e_z.by(i)
            sc.add("pe", 2, f)

            def f(e, s, pair=pair):
                need(e, e_z, s, pair)
                need(e, e_r, s + 1 if False else s)
                need(e, e_fmm, s)
                for c in range(2):
                    m = 2 * pair + c
                    i = e.activation(hd[m], dense[pair % 2][:, c * W:(c + 1) * W], ACT.Gelu,
                                     bias=b1[:, m:m + 1])
                e_h.by(i)
            sc.add("act", 2, f)

        def logits(pair):
            def f(e, s):
                need(e, e_fT, s)
                need(e, e_h, s, pair)
                for c in range(2):
                    m = 2 * pair + c
                    for b in range(NB):
                        i = e.matmul(s_lg[:, b * NF:(b + 1) * NF], hd[m][:, hs(b)], w2[:, m, :],
                                     start=(m == 0 and b == 0), stop=(m == HB - 1), skip_group_check=True)
                e_l.by(i)
            return f
        for pair in range(HB // 2):
            sc.add("pe", 1, logits(pair))

        sc.window(0.28, 0.31)

        def f(e, s):
            need(e, e_l, s)
            need(e, e_gw, s - 1)
            e_lb.by(e.tensor_tensor(lg[:, :, :, :].rearrange("p b h r -> p b (h r)"),
                                    s_lg.rearrange("p (b n) -> p b n", b=NB),
                                    b2[:, None, :].broadcast_to([P, NB, NF]), ALU.add))
            l3 = lg[:, :, :, :].rearrange("p b h r -> p (b h) r")
            w3 = gw[:, :, :, :].rearrange("p b h r -> p (b h) r")
            need(e, e_lb, s)
            e_mx.by(e.tensor_reduce(mx[:, :], l3, AX.X, ALU.max))
            need(e, e_mx, s)
            e_sub.by(e.tensor_tensor(l3, l3, mx[:, :, None].broadcast_to([P, NB * H, 3]), ALU.subtract))
            need(e, e_ex, s)
            e_sm.by(e.tensor_reduce(sm[:, :], l3, AX.X, ALU.add))
            need(e, e_sm, s)
            e_rs.by(e.reciprocal(rs[:, :], sm[:, :]))
            need(e, e_rs, s)
            need(e, e_m0, s - 1)
            need(e, e_m1, s - 1)
            need(e, e_m2, s - 1)
            e_gw.by(e.tensor_tensor(w3, l3, rs[:, :, None].broadcast_to([P, NB * H, 3]), ALU.mult))
        sc.add("dve", 1, f)

        def f(e, s):
            need(e, e_sub, s)
            e_ex.by(e.activation(lg[:, :, :, :], lg[:, :, :, :], ACT.Exp))
        sc.add("act", 1, f)

        sc.window(0.31, 0.47)
        for b in range(NB):
            def f(e, s, b=b):
                need(e, e_gw, s)
                need(e, e_ft, s, 3 * b + 2)
                need(e, e_Xy, s, b)
                e_m2.by(e.tensor_tensor(hv(y, b), hv(vtok, b), wide(gw[:, b, :, 2]), ALU.mult))
                e_m0.by(e.tensor_tensor(hv(ms, b), hv(ms, b), wide(gw[:, b, :, 0]), ALU.mult))
            sc.add("pool", 1, f)

            def f(e, s, b=b):
                need(e, e_gw, s)
                need(e, e_ft, s, 3 * b + 2)
                e_m1.by(e.tensor_tensor(hv(dl, b), hv(dl, b), wide(gw[:, b, :, 1]), ALU.mult))
                need(e, e_m1, s, b)
                need(e, e_m0, s, b)
                need(e, e_m2, s, b)
                e_a1.by(e.tensor_tensor(dl[:, b, :], dl[:, b, :], ms[:, b, :], ALU.add))
                need(e, e_a1, s, b)
                e_a2.by(e.tensor_tensor(dl[:, b, :], dl[:, b, :], y[:, b, :], ALU.add))
            sc.add("dve", 1, f)

            def f(e, s, b=b):
                need(e, e_a2, s, b)
                need(e, e_so, s, 0) if b else need(e, e_ka, s)
                e_sqo.by(e.activation(rl[:, :], dl[:, b, :], ACT.Square))
            sc.add("act", 1, f)

            def f(e, s, b=b):
                need(e, e_sqo, s, b)
                need(e, e_ro, s - 1, b)
                e_so.by(e.tensor_reduce(so[:, b, :], rl[:, :].rearrange("p (h d) -> p h d", h=H), AX.X, ALU.add))
            sc.add("dve", 1, f)

            def f(e, s, b=b):
                need(e, e_so, s, b)
                need(e, e_rro, s - 1, b)
                e_ro.by(e.activation(ro[:, b, :], so[:, b, :], ACT.Sqrt, bias=eps[:, 2:3], scale=1.0 / P))
            sc.add("act", 1, f)

            def f(e, s, b=b):
                need(e, e_ro, s, b)
                e_rro.by(e.reciprocal(rro[:, b, :], ro[:, b, :]))
                need(e, e_rro, s, b)
                need(e, e_a2, s, b)
                e_on.by(e.tensor_tensor(hv(dl, b), hv(dl, b), wide(rro[:, b, :]), ALU.mult))
            sc.add("dve", 1, f)

            def f(e, s, b=b):
                need(e, e_on, s, b)
                need(e, e_h, s, HB // 2 - 2 + b)
                for h in range(H):
                    i = e.transpose(dense[b][:, hs(h)], dl[:, b, hs(h)], ident)
                e_oTp.by(i)
            sc.add("pe", 1, f)

            def f(e, s, b=b):
                need(e, e_oTp, s, b)
                need(e, e_att, s - 1)
                e_oT.by(e.copy(oT[:, :, hs(b)], bh(dense[b])))
            sc.add("act", 1, f)

            def f(e, s, b=b):
                need(e, e_oT, s, b)
                for h in range(H):
                    i = e.matmul(dense[b][:, :], oT[:, h, hs(b)], wo[:, h, :], start=(h == 0), stop=(h == H - 1))
                e_att.by(i)
            sc.add("pe", 1, f)

            def f(e, s, b=b):
                need(e, e_att, s, b)
                need(e, e_res, s, b)
                e_xb.by(e.tensor_tensor(xb[:, b, :], xb[:, b, :], dense[b][:, :], ALU.add))
            sc.add("dve", 1, f)

        def f(e, s):
            need(e, e_xb, s)
            e.dma_start(out[:, bass.ds(s * P, P), :].rearrange("b p d -> p b d"), xb[:, :, :]).then_inc(stored, 16)
        sc.add("sp", 1, f)
        sc.flush()

        rest = (sf, sk, sc)
        first, second = convs[0] + convs[1], convs[2] + convs[3]
        sk.fill("dve", 0.63, first, rest, 0.0, 0.27)
        sk.fill("dve", 0.63, second, rest, 0.30, 0.93)

        loads = [
            (wq[:, :, :], w["wq"].rearrange("(k p) n -> p k n", p=P)),
            (wk[:, :, :], w["wk"].rearrange("(k p) n -> p k n", p=P)),
            (wv[:, :, :], w["wv"].rearrange("(k p) n -> p k n", p=P)),
            (wr[:, :, :], w["wrT"].rearrange("(k p) n -> p k n", p=P)),
            (wfk[:, :, :], w["wfkT"].rearrange("(k p) n -> p k n", p=P)),
            (wfv[:, :, :], w["wfvT"].rearrange("(k p) n -> p k n", p=P)),
            (cm[:, :, :], w["cm"].rearrange("(k p) n -> p k n", p=P)),
            (wo[:, :, :], w["wo"].rearrange("(k p) n -> p k n", p=P)),
            (w1[:, :, :], w["w1"][0:D, :].rearrange("(k p) n -> p k n", p=P)),
            (w1x[:, :], w["w1"][D:D + NF, :]),
            (km[:, :, :], w["km"].rearrange("(k p) n -> p k n", p=P)),
            (w2[:, :, :], w["w2"].rearrange("(k p) n -> p k n", p=P)),
            (b1[:, :], w["b1"]),
            (b2[:, :], w["b2"][None, :].broadcast_to([P, NF])),
            (wb[:, :, :], w["wb"].rearrange("(k p) n -> p k n", p=P)),
            (onw[:, :], w["onw"].rearrange("(p a) -> p a", a=1)),
            (mu[:, 0, :], w["mu_r"]),
            (mu[:, 1, :], w["mu_k"]),
            (cst[:, :], w["cst"]),
        ]
        for j, n in enumerate(("cq", "ck", "cv")):
            loads.append((cw[:, j, :, :], w[n].rearrange("(c p) k -> p c k", p=P)))
        for j, t in enumerate(TAPS):
            loads.append((mw[:, WOFF[j]:WOFF[j] + CB * t].rearrange("p (c k) -> p c k", k=t),
                          w[f"m{t}"].rearrange("(c p) k -> p c k", p=P)))
        NLOAD = 16 * len(loads)
        NSET = 7

        def start_load(e):
            for dst, src in loads:
                e.dma_start(dst, src).then_inc(wload, 16)

        def start_pool(e):
            for t in (S[:, :, :], halo[:, :, :, :], vT[:, :, :, :], xsh[:, :, :, :]):
                e.memset(t, 0.0).then_inc(setup, 1)
            for i, v in enumerate((1e-5, 1e-6, 1e-5)):
                e.memset(eps[:, i:i + 1], v).then_inc(setup, 1)

        def start_dve(e):
            for k in range(CB):
                e.tensor_scalar(wo[:, k, :], wo[:, k, :], onw[:, 0:1], None, ALU.mult).then_inc(wol, 1)

        order = {k: sorted([(p, 2, fn) for p, fn in sc.order(k)] + [(p, 1, fn) for p, fn in sk.order(k)]
                           + [(p, 0, fn) for p, fn in sf.order(k)], key=lambda t: (t[0], -t[1]))
                 for k in ("pe", "act", "dve", "pool", "sp")}

        def program(e, k):
            e.wait_ge(setup, NSET)
            if k != "sp":
                e.wait_ge(wload, NLOAD)
            if k == "dve":
                start_dve(e)
            if k == "pe":
                e.wait_ge(wol, CB)
            def iteration(i, ages):
                if k == "dve":
                    chain.restart(e, isinstance(i, int) and i == 0)
                for _, age, fn in order[k]:
                    if age in ages:
                        fn(e, i - age)

            iteration(0, (0,))
            iteration(1, (0, 1))
            iteration(2, (0, 1, 2))
            with e.Fori(3, NS) as i:
                iteration(i, (0, 1, 2))
            iteration(NS, (1, 2))
            iteration(NS + 1, (2,))
            if k == "sp":
                e.wait_ge(stored, 16 * NS)

        block = ctx.enter_context(nc.Block())

        @block.sync
        def _(e):
            start_load(e)
            program(e, "sp")

        @block.gpsimd
        def _(e):
            start_pool(e)
            program(e, "pool")

        @block.vector
        def _(e):
            program(e, "dve")

        @block.scalar
        def _(e):
            program(e, "act")

        @block.tensor
        def _(e):
            program(e, "pe")

        for name, ev in events:
            assert ev.seen == 4 * ev.n, (name, ev.seen, ev.n)


def kernel(**inputs):
    import numpy as np
    import concourse.bacc as bacc
    from concourse.bass_utils import run_bass_kernel_spmd

    cst = np.zeros((P, C_ONE + 2), np.float32)
    r, c = np.arange(P)[:, None], np.arange(P)[None, :]
    cst[:, C_UP * P:(C_UP + 1) * P] = r < c
    cst[:, C_UPI * P:(C_UPI + 1) * P] = r <= c
    cst[:, C_ID * P:(C_ID + 1) * P] = r == c
    for i, k in enumerate(LEVELS):
        n = np.arange(HP)[None, :] // k
        cst[:, C_LEV + i * HP:C_LEV + (i + 1) * HP] = (r // (2 * k) == n) & (r // k % 2 == 1)
    cst[:, C_ONE:] = 1.0

    a = {k: np.asarray(v) for k, v in inputs.items()}
    A = "L0_attn_"
    arrays = {
        "x": a[A + "hidden_states"], "wq": a[A + "Wq"], "wk": a[A + "Wk"], "wv": a[A + "Wv"], "wb": a[A + "Wb"],
        "cq": a[A + "conv_q_w"], "ck": a[A + "conv_k_w"], "cv": a[A + "conv_v_w"],
        "m3": a[A + "ms_w3"], "m15": a[A + "ms_w15"], "m31": a[A + "ms_w31"],
        "km": a[A + "kernel_mix_w"], "cm": a[A + "channel_mixer_w"],
        "w1": a[A + "fusion_w1"], "b1": a[A + "fusion_b1"].reshape(HB, P).T, "w2": a[A + "fusion_w2"], "b2": a[A + "fusion_b2"],
        "onw": a[A + "o_norm_w"], "wo": a[A + "Wo"],
        "wrT": a["L0_ffn_W_r"].T, "wfkT": a["L0_ffn_W_k"].T, "wfvT": a["L0_ffn_W_v"].T,
        "mu_r": a["L0_ffn_mu_r"].reshape(CB, P).T, "mu_k": a["L0_ffn_mu_k"].reshape(CB, P).T, "cst": cst,
    }
    arrays = {k: np.ascontiguousarray(v) for k, v in arrays.items()}
    nc = bacc.Bacc("TRN2", target_bir_lowering=False, num_devices=1)
    arrays = {f"in_{k}": v for k, v in arrays.items()}
    aps = {k[3:]: nc.dram_tensor(k, v.shape, F32, kind="ExternalInput").ap() for k, v in arrays.items()}
    out = nc.dram_tensor("out", arrays["in_x"].shape, F32, kind="ExternalOutput").ap()
    x = aps.pop("x")
    build(nc, x, out, aps)
    r = run_bass_kernel_spmd(nc, [arrays], core_ids=[0])
    return r.results[0]["out"]
```

```python
from contextlib import ExitStack
from math import floor

import concourse.bass as bass
from concourse import mybir

F32 = mybir.dt.float32
BF16 = mybir.dt.bfloat16
ALU = mybir.AluOpType
ACT = mybir.ActivationFunctionType
AX = mybir.AxisListType

P = 128
H = 4
D = H * P
NB = 2
W = NB * P
CB = D // P
HID = 2 * D
HB = HID // P
TAPS = (3, 15, 31)
SK = 4
SH = SK - 1
VH = max(TAPS) - 1
NF = 3 * H
PARTS = 3
NROW = PARTS * PARTS * NF
SQ = 32
LEVELS = [1 << i for i in range(6)]
WOFF = [0, TAPS[0] * CB, (TAPS[0] + TAPS[1]) * CB]
HP = P // 2
C_UP, C_UPI, C_ID = range(3)
C_LEV = 3 * P
C_PART = C_LEV + len(LEVELS) * HP
C_ONE = C_PART + PARTS


AT = {
    "x": (0.2789,),
    "layer norm": (0.0092, 0.1785, 0.2570, 0.3347),
    "norm transposed": (0.3176, 0.3253, 0.5373, 0.4275, 0.5477, 0.5753),
    "projections": (0.7111, 0.0590, 0.6984, 0.6994, 0.7744, 0.8598, 0.8356, 0.7749, 0.1714, 0.7583, 0.8264,
        0.7755, 0.8766, 0.9407, 0.8293, 0.6192, 0.8297, 0.8799, 0.8344, 0.8849, 0.9427, 0.8804, 0.7950,
        0.8798, 0.9182, 0.9400, 0.9031, 0.9427, 0.8926, 0.9373, 0.9537, 1.1244, 1.0425, 1.0207, 1.1082,
        0.9195, 0.9725, 1.0433, 1.1939, 1.0587, 1.0464, 1.1328),
    "beta and q's norms": (0.9451, 0.9485),
    "residual x": (0.9330,),
    "shift": (0.3593,),
    "Gram": (-0.1055, -0.0287, -0.0534, -0.0108, 0.0016, 0.0196, 0.0116, 0.0203, 0.0218, -0.0187, 0.0219,
        0.0015, 0.0256, 0.0300, 0.0269, 0.0397, 0.0711),
    "inverse": (0.0230, 0.0261, 0.0500, 0.0516, -0.2140, 0.0262, 0.1588, 0.0527, 0.0512, 0.0761, 0.0362,
        0.0638, 0.0964, 0.0805, 0.0674, 0.0966, 0.0720, 0.1011, 0.1069, 0.1574, 0.0999, 0.1374, 0.1885,
        0.1303, 0.1278, 0.1823, 0.1632, 0.2394, 0.1831, 0.2847, 0.2168, 0.2242, 0.3219, 0.2862, 0.2393,
        0.3317, 0.2567, 0.3578, 0.2699, 0.3495, 0.3383, 0.3235, 0.3792, 0.3825, 0.3230, 0.3636, 0.3474,
        0.3930, 0.3238, 0.3842, 0.4244, 0.4207, 0.4262, 0.4322, 0.5337, 0.4599, 0.6141, 0.5245),
    "v tokens": (0.3472, 0.4453, 0.4981, 0.5483, 0.4651, 0.5381),
    "recurrence": (0.6022, 0.4670, 0.5399, 0.6469, 0.4885, 0.6395, 0.6668, 0.4884, 0.6788, 0.6425, 0.7249,
        0.6672, 0.6973, 0.6189, 0.7402, 0.7585, 0.7964, 0.7211, 0.8243, 0.7597, 0.8320, 0.7835, 0.8724,
        0.8851, 0.8853, 1.0032),
    "mix in": (0.4647,),
    "FFN": (0.6259, 0.4713, 0.4901, 0.6735, 0.4924, 0.5376, 0.6844, 0.7241, 0.8078, 0.7755, 0.8853, 0.8843,
        1.0055, 1.0590),
    "first taps": (0.1438, 0.1498, 0.2358, 0.3782),
    "kernel mix": (0.2074, 0.2450, 0.2768, 0.4833, 0.8408, 0.7989, 0.9987, 0.9902),
    "taps": (0.0620, 0.0656, 0.0691, 0.0761, 0.0847, 0.0860, 0.0910, 0.0941, 0.0970, 0.0999, 0.1016, 0.1150,
        0.1260, 0.1323, 0.1323, 0.1372, 0.1455, 0.1547, 0.1695, 0.1798, 0.1840, 0.1844, 0.1869, 0.1872,
        0.1881, 0.2093, 0.2144, 0.2206, 0.2243, 0.2301, 0.2306, 0.2321, 0.2353, 0.2410, 0.2854, 0.3145,
        0.3233, 0.3252, 0.3254, 0.3390, 0.3533, 0.3629, 0.3675, 0.3679, 0.3683, 0.3847, 0.3887, 0.3924,
        0.3955, 0.4083, 0.4358, 0.4383, 0.4392, 0.4481, 0.4495, 0.4498, 0.4504, 0.4541, 0.4598, 0.4680,
        0.4685, 0.4692, 0.4719, 0.4808, 0.4838, 0.4892, 0.5002, 0.5012, 0.5107, 0.5123, 0.5197, 0.5253,
        0.5257, 0.5301, 0.5400, 0.5406, 0.5418, 0.5484, 0.5549, 0.5554, 0.5608, 0.5611, 0.5616, 0.5728,
        0.5761, 0.5767, 0.5988, 0.6002, 0.6003, 0.6080, 0.6086, 0.6093, 0.6096, 0.6166, 0.6214, 0.6218,
        0.6231, 0.6336, 0.6349, 0.6379, 0.6396, 0.6477, 0.6513, 0.6564, 0.6613, 0.6619, 0.6628, 0.6639,
        0.6814, 0.6887, 0.6963, 0.6968, 0.7011, 0.7072, 0.7123, 0.7139, 0.7362, 0.7370, 0.7411, 0.7467,
        0.7517, 0.7535, 0.7639, 0.7686, 0.7783, 0.7795, 0.7797, 0.7812, 0.7824, 0.7826, 0.7828, 0.7853,
        0.7958, 0.7969, 0.7982, 0.7990, 0.8003, 0.8054, 0.8096, 0.8202, 0.8204, 0.8235, 0.8244, 0.8247,
        0.8255, 0.8502, 0.8536, 0.8626, 0.8748, 0.8754, 0.8755, 0.8813, 0.8824, 0.8838, 0.8857, 0.8975,
        0.9009, 0.9048, 0.9068, 0.9102, 0.9186, 0.9280, 0.9326, 0.9364, 0.9369, 0.9405, 0.9450, 0.9460,
        0.9462, 0.9600, 0.9635, 0.9676, 0.9685, 0.9685, 0.9781, 0.9797, 0.9846, 0.9868, 0.9890, 0.9899,
        0.9927, 0.9961, 0.9978, 0.9993),
    "channel mix": (0.0205, 0.0555, 0.0298, 0.0634, 0.0769, 0.0326, 0.0864, 0.0379, 0.0547, 0.1178),
    "fusion": (0.0611, 0.1474, 0.0634, 0.1572, 0.1198, 0.1796, 0.1497, 0.1953, 0.0742, 0.0812, 0.1568,
        0.1809),
    "softmax": (0.2507, 0.2627, 0.2635, 0.2902, 0.2913, 0.2987, 0.1968),
    "out": (0.1826, 0.2635, 0.3483, 0.3513, 0.2873, 0.3058, 0.3738, 0.3532, 0.4052, 0.3879, 0.4951, 0.4803,
        0.2724, 0.2652, 0.3613, 0.3796, 0.3709, 0.4216, 0.4352, 0.4385, 0.5414, 0.4578, 0.5884, 0.5375,
        0.4531),
}


class Event:

    def __init__(self, sem, n):
        self.sem, self.n, self.seen = sem, n, 0

    def at(self, s, i):
        return s * self.n + i + 1

    def by(self, ins):
        self.seen += 1
        ins.then_inc(self.sem, 1)


def need(e, ev, s, i=None):
    if isinstance(s, int) and s < 0:
        return
    e.wait_ge(ev.sem, ev.at(s, ev.n - 1 if i is None else i))


class Chain:

    def __init__(self, sem):
        self.sem, self.n = sem, 0

    def restart(self, e, first):
        if not first:
            e.wait_ge(self.sem, self.n)
            e.sem_clear(self.sem)
        self.n = 0

    def link(self, ins):
        self.n += 1
        ins.then_inc(self.sem, 1)
        return self.n

    def after(self, e, n):
        e.wait_ge(self.sem, n)


class Schedule:

    def __init__(self, age):
        self.age, self.items, self.places = age, [], {}

    def at(self, stage):
        self.stage = stage
        self.places.setdefault(stage, iter(AT[stage]))

    def add(self, eng, fn):
        self.items.append((next(self.places[self.stage]), eng, fn))

    def order(self, eng):
        return [(p - floor(p), self.age + floor(p), fn) for p, k, fn in self.items if k == eng]


def build(nc, x, out, w):
    NS = x.shape[1] // P
    with ExitStack() as ctx:
        def sb(name, *shape, dtype=F32):
            return ctx.enter_context(nc.sbuf_tensor(name, list(shape), dtype))

        def bank(name):
            return ctx.enter_context(nc.psum_tensor(name, [P, 512], F32))

        def event(name, n):
            ev = Event(ctx.enter_context(nc.semaphore(name)), n)
            events.append((name, ev))
            return ev

        events = []

        wq, wk, wv = (sb(n, P, CB, D) for n in ("wq", "wk", "wv"))
        wr, wfk, wfv = (sb(n, P, CB, D) for n in ("wr", "wfk", "wfv"))
        cm, wo = sb("cm", P, CB, D), sb("wo", P, CB, D)
        w1 = sb("w1", P, CB, HID)
        w1x = sb("w1x", NROW, HID, dtype=BF16)
        km = sb("km", P, 3, P)
        w2 = sb("w2", P, HB, NF)
        b1 = sb("b1", P, HB)
        b2 = sb("b2", P, NF)
        wb = sb("wb", P, CB, H)
        onw = sb("onw", P, 1)
        mu = sb("mu", P, 2, CB)
        cw = sb("cw", P, 3, CB, SK)
        mw = sb("mw", P, sum(TAPS) * CB)
        cst = sb("cst", P, C_ONE + 2)
        eps = sb("eps", P, 3)
        ident = cst[:, C_ID * P:(C_ID + 1) * P]
        ones = cst[:, C_ONE:C_ONE + 1]

        def mask(i):
            return cst[:, i * P:(i + 1) * P][:, None, :].broadcast_to([P, H, P])

        def level_mask(l):
            k = LEVELS[l]
            m = cst[:, C_LEV + l * HP:C_LEV + (l + 1) * HP].rearrange("p (n k) -> p n k", k=k)
            return m[:, None, :, :].broadcast_to([P, H, HP // k, k])

        def even(t, k):
            return t.rearrange("p (n k) -> p n k", k=2 * k)[:, :, 0:k]

        xa = sb("xa", P, NB, D)
        xb = sb("xb", P, NB, D)
        xnT = sb("xnT", P, CB, W)
        xsh = sb("xsh", P, CB, NB, 1 + P)
        xr, xk = sb("xr", P, CB, W), sb("xk", P, CB, W)
        rl = sb("rl", P, 2 * W)
        ka = sb("ka", P, CB, W)
        th = sb("th", P, D)
        raw = [sb(f"raw{i}", P, 2, NB, SH + P) for i in range(2)]
        halo = sb("halo", P, 3 * CB, NB, SH)
        qT, kT = sb("qT", P, CB, W), sb("kT", P, CB, W)
        vT = sb("vT", P, CB, NB, VH + P)
        ktok, vtok = sb("ktok", P, NB, D), sb("vtok", P, NB, D)
        y, u = sb("y", P, NB, D), sb("u", P, NB, D)
        Bm, Y, X, aT = (sb(n, P, NB, D) for n in ("Bm", "Y", "X", "aT"))
        Wm = sb("Wm", P, NB, H * HP)
        S = sb("S", P, NB, D)
        dl = sb("dl", P, NB, D)
        my = [sb(f"my{i}", P, 3, W) for i in range(2)]
        ym = sb("ym", P, CB, W)
        ms = sb("ms", P, NB, D)
        bst, mv = sb("bst", P, NB, 6), sb("mv", P, NB, 2)
        std, rstd, nmr = sb("std", P, NB), sb("rstd", P, NB), sb("nmr", P, NB)
        nrm, rn = sb("nrm", P, NB, 2 * H), sb("rn", P, NB, 2 * H)
        nk = sb("nk", P, NB, H)
        bt, gt, g = sb("bt", P, NB, H), sb("gt", P, NB, H), sb("g", P, NB, H)
        ft, ftT = sb("ft", P, NB, NF), sb("ftT", NROW, W, dtype=BF16)
        fparts, frest = sb("fparts", P, NB, PARTS, PARTS, NF, dtype=BF16), sb("frest", P, NB, NF)
        ident16 = sb("ident16", P, P, dtype=BF16)
        lg, gw = sb("lg", P, NB, H, 3), sb("gw", P, NB, H, 3)
        mx, sm, rs = sb("mx", P, NB * H), sb("sm", P, NB * H), sb("rs", P, NB * H)
        so, ro, rro = sb("so", P, NB, H), sb("ro", P, NB, H), sb("rro", P, NB, H)
        oT = sb("oT", P, CB, W)
        sq = u[:, :, :].rearrange("p b (c w) -> p (b c) w", w=W)
        hd = [t[:, c, :] for t in (xr, xk) for c in range(CB)]

        front = [bank(f"front{i}") for i in range(2)]
        dense = [bank(f"dense{i}") for i in range(2)]
        cell = [bank(f"cell{b}") for b in range(NB)]
        turn = bank("turn")
        small = bank("small")
        s_norm = front[0][:, 0:NB * H]
        s_beta = front[0][:, 32:32 + NB * H]
        s_ft = small[0:NROW, 64:64 + W]
        s_mix = small[:, 64:64 + W]
        s_lg = small[:, 384:384 + NB * NF]

        def hv(t, b):
            return t[:, b, :].rearrange("p (h d) -> p h d", h=H)

        def bh(t):
            return t[:, :].rearrange("p (h d) -> p h d", h=H)

        def wide(col):
            return col[:, :, None].broadcast_to([P, H, P])

        def hs(h):
            return slice(h * P, (h + 1) * P)

        held = ctx.enter_context(nc.semaphore("held"))

        def hold(e):
            e.sem_inc(held, 1)

        chain = Chain(ctx.enter_context(nc.semaphore("dve_chain")))
        front_loaded = ctx.enter_context(nc.semaphore("front_loaded"))
        loaded = ctx.enter_context(nc.semaphore("loaded"))
        setup = ctx.enter_context(nc.semaphore("setup"))
        scaled = ctx.enter_context(nc.semaphore("weights_scaled"))
        xa_in = ctx.enter_context(nc.semaphore("xa_in"))
        xb_in = ctx.enter_context(nc.semaphore("xb_in"))
        stored = ctx.enter_context(nc.semaphore("stored"))

        sf, sk, sc = Schedule(0), Schedule(1), Schedule(2)

        e_stat, e_agg = event("e_stat", NB), event("e_agg", NB)
        e_std, e_rstd, e_nmr = event("e_std", 1), event("e_rstd", 1), event("e_nmr", 1)
        e_xn, e_xT, e_xnT = event("e_xn", NB), event("e_xT", NB), event("e_xnT", NB)
        e_proj, e_raw = event("e_proj", 6), event("e_raw", 6)
        e_hin, e_hout = event("e_hin", 6), event("e_hout", 6)
        e_vh = event("e_vh", 1)
        e_cv = event("e_cv", 6 * 2)
        e_act = event("e_act", 6)
        e_c0, e_t0 = event("e_c0", 6), event("e_t0", H)
        e_xcp = event("e_xcp", 2)
        e_msc = event("e_msc", 3 * H)
        e_tk, e_sqq = event("e_tk", 2 * NB), event("e_sqq", 1)
        e_S, e_KTu = event("e_S", NB), event("e_KTu", NB)
        e_o = event("e_o", NB)
        e_xb = event("e_xb", NB)
        e_gr, e_qk = event("e_gr", NB), event("e_qk", NB)

        e_fmm, e_frl, e_ka = event("e_fmm", 2), event("e_frl", 2), event("e_ka", 2)
        e_dx, e_xrk = event("e_dx", 1), event("e_xrk", 2 * CB)
        e_r, e_th = event("e_r", NB), event("e_th", NB)
        e_kv, e_gate = event("e_kv", NB), event("e_gate", NB)
        e_res = event("e_res", NB)
        e_nn, e_bm = event("e_nn", 1), event("e_bm", 1)
        e_nrm = event("e_nrm", 2)
        e_rn, e_bt, e_b2, e_gt, e_g = (event(n, 1) for n in ("e_rn", "e_bt", "e_b2", "e_gt", "e_g"))
        e_tT = event("e_tT", 2 * NB)
        e_vn = event("e_vn", NB)
        e_B, e_aT = event("e_B", NB * H), event("e_aT", NB)
        e_Yo = event("e_Yo", NB)
        NL = len(LEVELS)
        e_tcp, e_dc, e_msb = event("e_tcp", 2 * NB), event("e_dc", NB), event("e_msb", NB)
        e_BT = event("e_BT", NB)
        e_Wp, e_W = event("e_Wp", NB * (NL - 1)), event("e_W", NB * NL)
        e_Xs, e_Xp, e_X = event("e_Xs", NB * (NL - 1)), event("e_Xp", NB), event("e_X", NB)
        e_Zp, e_Y = event("e_Zp", NB * (NL - 1)), event("e_Y", NB * NL)
        e_KS, e_y, e_Xy, e_uf, e_u = (event(n, NB) for n in ("e_KS", "e_y", "e_Xy", "e_uf", "e_u"))
        e_first, e_Bu, e_Bc, e_all = (event(n, NB) for n in ("e_first", "e_Bu", "e_Bc", "e_all"))
        e_d = event("e_d", NB)
        e_km, e_ym = event("e_km", H), event("e_ym", H)
        e_cm, e_ms = event("e_cm", NB), event("e_ms", NB)
        e_fp, e_fT = event("e_fp", NB), event("e_fT", NB)
        e_f1, e_f2, e_f3, e_f4 = (event(n, 1) for n in ("e_f1", "e_f2", "e_f3", "e_f4"))
        e_z, e_h, e_l = event("e_z", HB // 2), event("e_h", HB // 2), event("e_l", HB // 2)
        e_lb, e_mx, e_sub, e_ex, e_sm, e_rs, e_gw = (
            event(n, 1) for n in ("e_lb", "e_mx", "e_sub", "e_ex", "e_sm", "e_rs", "e_gw"))
        e_m0, e_m1, e_m2 = event("e_m0", NB), event("e_m1", NB), event("e_m2", NB)
        e_a1, e_a2 = event("e_a1", NB), event("e_a2", NB)
        e_so, e_ro, e_rro, e_on = (event(n, NB) for n in ("e_so", "e_ro", "e_rro", "e_on"))
        e_oTp, e_oT, e_att = event("e_oTp", NB), event("e_oT", NB), event("e_att", NB)

        sf.at("x")

        def f(e, s):
            need(e, e_xT, s - 1)
            e.dma_start(xa[:, :, :], x[:, bass.ds(s * P, P), :].rearrange("b p d -> p b d")).then_inc(xa_in, 16)
        sf.add("sp", f)

        sf.at("layer norm")

        def f(e, s):
            e.wait_ge(xa_in, s * 16 + 16)
            for b in range(NB):
                e_stat.by(e.bn_stats(bst[:, b, :], xa[:, b, :]))
            for b in range(NB):
                need(e, e_stat, s, b)
                if b == 0:
                    need(e, e_xn, s - 1)
                hold(e)
                e_agg.by(e.bn_aggr(mv[:, b, :], bst[:, b, :]))
        sf.add("dve", f)

        def f(e, s):
            need(e, e_agg, s)
            need(e, e_rstd, s - 1)
            e_std.by(e.activation(std[:, :], mv[:, :, 1], ACT.Sqrt, bias=eps[:, 0:1]))
        sf.add("act", f)

        def f(e, s):
            need(e, e_std, s)
            e_rstd.by(e.reciprocal(rstd[:, :], std[:, :]))
        sf.add("dve", f)

        def f(e, s):
            need(e, e_rstd, s)
            e_nmr.by(e.scalar_tensor_tensor(nmr[:, :], mv[:, :, 0], -1.0, rstd[:, :], ALU.mult, ALU.mult))
        sf.add("dve", f)

        sf.at("norm transposed")
        for b in range(NB):
            def f(e, s, b=b):
                e.wait_ge(xa_in, s * 16 + 16)
                need(e, e_nmr, s)
                e_xn.by(e.activation(xa[:, b, :], xa[:, b, :], ACT.Identity, bias=nmr[:, b:b + 1],
                                     scale=rstd[:, b:b + 1]))
            sf.add("act", f)

            def f(e, s, b=b):
                need(e, e_xn, s, b)
                if b == 0:
                    need(e, e_bt, s - 1)
                    need(e, e_nrm, s - 1, 0)
                else:
                    need(e, e_raw, s - 1, 5)
                for c in range(CB):
                    i = e.transpose(front[b][:, hs(c)], xa[:, b, hs(c)], ident)
                e_xT.by(i)
            sf.add("pe", f)

            def f(e, s, b=b):
                need(e, e_xT, s, b)
                need(e, e_xcp, s - 1)
                need(e, e_bm, s - 1)
                e_xnT.by(e.copy(xnT[:, :, hs(b)], bh(front[b])))
            sf.add("act", f)

        for pair in range(6):
            j, c0 = pair // 2, 2 * (pair % 2)
            wt, r = (wq, wk, wv)[j], raw[pair % 2]
            sf.at("projections")

            def f(e, s, pair=pair, wt=wt, c0=c0):
                if pair == 0:
                    need(e, e_xnT, s)
                if pair < 2:
                    need(e, e_xnT, s, pair)
                else:
                    need(e, e_raw, s, pair - 2)
                for c in range(2):
                    for k in range(CB):
                        i = e.matmul(front[pair % 2][:, c * W:(c + 1) * W], wt[:, k, hs(c0 + c)], xnT[:, k, :],
                                     start=(k == 0), stop=(k == CB - 1))
                e_proj.by(i)
            sf.add("pe", f)

            def f(e, s, pair=pair, r=r):
                need(e, e_cv, s if pair >= 2 else s - 1, 2 * ((pair - 2) % 6) + 1)
                if pair == 4:
                    need(e, e_msc, s - 1)
                    need(e, e_tk, s - 1)
                    hold(e)
                    e_vh.by(e.tensor_copy(vT[:, :, :, 0:VH], vT[:, :, :, P:P + VH]))
                need(e, e_hout, s - 1, pair)
                hold(e)
                e_hin.by(e.tensor_copy(r[:, :, :, 0:SH],
                                       halo[:, 2 * pair:2 * pair + 2, :, :]))
            sf.add("pool", f)

            def f(e, s, pair=pair, r=r):
                need(e, e_proj, s, pair)
                if pair >= 2:
                    need(e, e_cv, s, 2 * (pair - 2) + 1)
                    need(e, e_hout, s, pair - 2)
                else:
                    need(e, e_cv, s - 1, 2 * (pair + 4) + 1)
                    need(e, e_hout, s - 1, pair + 4)
                for c in range(2):
                    i = e.copy(r[:, c, :, SH:SH + P],
                               front[pair % 2][:, c * W:(c + 1) * W].rearrange("p (b t) -> p b t", b=NB))
                e_raw.by(i)
            sf.add("act", f)

            def f(e, s, pair=pair, r=r):
                need(e, e_raw, s, pair)
                need(e, e_hin, s, pair)
                hold(e)
                e_hout.by(e.tensor_copy(halo[:, 2 * pair:2 * pair + 2, :, :], r[:, :, :, P:P + SH]))
            sf.add("pool", f)

            def dst(c, j=j, c0=c0):
                if j == 2:
                    return vT[:, c0 + c, :, VH:VH + P]
                return (qT, kT)[j][:, c0 + c, :].rearrange("p (b t) -> p b t", b=NB)

            def f(e, s, pair=pair, r=r, j=j, c0=c0, dst=dst):
                need(e, e_raw, s, pair)
                need(e, e_hin, s, pair)
                if pair == 0:
                    need(e, e_o, s - 1)
                    need(e, e_qk, s - 1)
                    need(e, e_nn, s - 1)
                if pair == 2:
                    need(e, e_KTu, s - 1)
                    need(e, e_tk, s - 1)
                if pair == 4:
                    need(e, e_vh, s)
                for c in range(2):
                    i = e.activation(dst(c), r[:, c, :, 0:P], ACT.Copy, scale=cw[:, j, c0 + c, 0:1])
                e_c0.by(i)
            sf.add("act", f)

            def f(e, s, pair=pair, r=r, j=j, c0=c0, dst=dst):
                need(e, e_c0, s, pair)
                last = {}
                for t in range(1, SK):
                    for c in range(2):
                        src, wc = r[:, c, :, t:t + P], cw[:, j, c0 + c, t:t + 1]
                        if t > 1:
                            chain.after(e, last[c])
                        i = e.scalar_tensor_tensor(dst(c), src, wc, dst(c), ALU.mult, ALU.add)
                        if t < SK - 1:
                            last[c] = chain.link(i)
                        else:
                            e_cv.by(i)
            sf.add("dve", f)

            def f(e, s, pair=pair, dst=dst):
                need(e, e_cv, s, 2 * pair + 1)
                for c in range(2):
                    i = e.activation(dst(c), dst(c), ACT.Silu)
                e_act.by(i)
            sf.add("act", f)

        sf.at("beta and q's norms")

        def f(e, s):
            need(e, e_act, s, 1)
            need(e, e_KTu, s - 1)
            e_sqq.by(e.activation(sq, qT[:, :, :], ACT.Square))
        sf.add("act", f)

        def f(e, s):
            need(e, e_raw, s, 4)
            for b in range(NB):
                for k in range(CB):
                    i = e.matmul(s_beta[:, b * H:(b + 1) * H], xnT[:, k, hs(b)], wb[:, k, :],
                                 start=(k == 0), stop=(k == CB - 1))
            e_bm.by(i)
            need(e, e_sqq, s)
            for b in range(NB):
                for h in range(H):
                    n = b * H + h
                    i = e.matmul(s_norm[:, n:n + 1], sq[:, h, hs(b)], ones, start=True, stop=True)
            e_nn.by(i)
        sf.add("pe", f)

        sk.at("residual x")

        def f(e, s):
            if not (isinstance(s, int) and s == 0):
                e.wait_ge(stored, s * 16)
            e.dma_start(xb[:, :, :], x[:, bass.ds(s * P, P), :].rearrange("b p d -> p b d")).then_inc(xb_in, 16)
        sk.add("sp", f)

        sk.at("shift")

        def f(e, s):
            need(e, e_xnT, s)
            need(e, e_z, s - 1)
            need(e, e_xrk, s - 1)
            hold(e)
            e_xcp.by(e.tensor_copy(xsh[:, :, :, 0:1], xsh[:, :, :, P:P + 1]))
            need(e, e_xcp, s, 0)
            hold(e)
            e_xcp.by(e.tensor_copy(xsh[:, :, :, 1:1 + P], xnT[:, :, :].rearrange("p c (b t) -> p c b t", b=NB)))
        sk.add("pool", f)

        def token_major(b, j):
            tok, n = (ktok, vtok)[j], NB * j + b

            def f(e, s):
                need(e, e_act, s, 3 + 2 * j)
                if n == 0:
                    need(e, e_Bc, s - 1)
                else:
                    need(e, e_tk, s, n - 1)
                for h in range(H):
                    t = kT[:, h, hs(b)] if j == 0 else vT[:, h, b, VH:VH + P]
                    i = e.transpose(turn[:, hs(h)], t, ident)
                e_tT.by(i)
            sk.add("pe", f)

            def f(e, s):
                need(e, e_tT, s, n)
                need(e, (e_KTu, e_m2)[j], s - 1, b)
                e_tcp.by(e.copy(tok[:, b, :], turn[:, :]))
                need(e, e_tcp, s, n)
                need(e, e_f2, s - 1) if j else need(e, e_nrm, s - 1)
                for h in range(H):
                    func, total = ((ACT.Square, nk[:, b, h:h + 1]),
                                   (ACT.Abs, ft[:, b, 2 * H + h:2 * H + h + 1]))[j]
                    i = e.activation(turn[:, hs(h)], turn[:, hs(h)], func, accum_out=total)
                e_tk.by(i)
            sk.add("act", f)

        sk.at("Gram")
        for b in range(NB):
            token_major(b, 0)

        def f(e, s):
            need(e, e_bm, s)
            need(e, e_nn, s)
            need(e, e_b2, s - 1)
            e_bt.by(e.activation(bt[:, :, :], s_beta.rearrange("p (b n) -> p b n", b=NB), ACT.Tanh, scale=0.5))
            need(e, e_d, s - 1)
            need(e, e_vn, s - 1)
            e_nrm.by(e.activation(nrm[:, :, 0:H], s_norm.rearrange("p (b n) -> p b n", b=NB), ACT.Sqrt,
                                  bias=eps[:, 1:2]))
            need(e, e_tk, s, NB - 1)
            e_nrm.by(e.activation(nrm[:, :, H:2 * H], nk[:, :, :], ACT.Sqrt, bias=eps[:, 1:2]))
        sk.add("act", f)

        def f(e, s):
            need(e, e_bt, s)
            e_b2.by(e.tensor_scalar(gt[:, :, :], bt[:, :, :], 0.5, 0.5, ALU.mult, ALU.add))
        sk.add("dve", f)

        def f(e, s):
            need(e, e_nrm, s)
            e_rn.by(e.reciprocal(rn[:, :, :], nrm[:, :, :]))
        sk.add("dve", f)

        def f(e, s):
            need(e, e_rn, s)
            need(e, e_b2, s)
            e_gt.by(e.tensor_tensor(gt[:, :, :], gt[:, :, :], rn[:, :, H:2 * H], ALU.mult))
        sk.add("dve", f)

        def f(e, s):
            need(e, e_gt, s)
            need(e, e_B, s - 1)
            need(e, e_u, s - 1)
            e_g.by(e.tensor_tensor(g[:, :, :], gt[:, :, :], rn[:, :, H:2 * H], ALU.mult))
        sk.add("dve", f)

        for b in range(NB):
            def f(e, s, b=b):
                if b == 0:
                    need(e, e_act, s, 3)
                need(e, e_S, s - 1, b)
                for h in range(H):
                    i = e.matmul(cell[b][:, hs(h)], kT[:, h, hs(b)], kT[:, h, hs(b)], start=True, stop=True)
                e_gr.by(i)
            sk.add("pe", f)

            def f(e, s, b=b):
                need(e, e_gr, s, b)
                need(e, e_g, s)
                need(e, e_Bu, s - 1, b)
                for h in range(H):
                    e_B.by(e.scalar_tensor_tensor(Bm[:, b, hs(h)], cell[b][:, hs(h)], g[:, b, h:h + 1],
                                                  cst[:, C_UP * P:(C_UP + 1) * P], ALU.mult, ALU.mult))
            sk.add("dve", f)

        for b in range(NB):
            def f(e, s, b=b):
                need(e, e_B, s, H * (b + 1) - 1)
                for h in range(H):
                    i = e.matmul(cell[b][:, hs(h)], kT[:, h, hs(b)], qT[:, h, hs(b)], start=True, stop=True)
                e_qk.by(i)
            sk.add("pe", f)

            def f(e, s, b=b):
                need(e, e_qk, s, b)
                need(e, e_o, s - 1, b)
                e_aT.by(e.tensor_tensor(hv(aT, b), bh(cell[b]), mask(C_UPI), ALU.mult))
            sk.add("dve", f)

        sk.at("inverse")
        for l in range(NL):
            for b in range(NB):
                n = NB * l + b

                k = LEVELS[l]
                if l == 0:
                    def f(e, s, b=b):
                        need(e, e_B, s, H * (b + 1) - 1)
                        need(e, e_all, s - 1, b)
                        e_BT.by(e.transpose(X[:, b, :], Bm[:, b, :]))
                    sk.add("dve", f)
                else:
                    def f(e, s, b=b, n=n, k=k, l=l):
                        if l == 1:
                            need(e, e_aT, s, b)
                        need(e, e_Y, s, n - NB)
                        for h in range(H):
                            i = e.matmul(cell[b][:, h * HP:(h + 1) * HP].rearrange("p (n k) -> p n k", k=k),
                                         Bm[:, b, hs(h)], even(Y[:, b, hs(h)], k), start=True, stop=True)
                        e_Wp.by(i)
                    sk.add("pe", f)

                def f(e, s, l=l, b=b, n=n):
                    k = LEVELS[l]
                    if l == 0:
                        need(e, e_BT, s, b)
                        need(e, e_Zp, s - 1, NB * (NL - 2) + b)
                        src = even(X[:, b, :], 1).rearrange("p (h n) k -> p h n k", h=H)
                    else:
                        need(e, e_Wp, s, n - NB)
                        src = cell[b][:, 0:H * HP].rearrange("p (h n k) -> p h n k", h=H, k=k)
                    e_W.by(e.tensor_tensor(Wm[:, b, :].rearrange("p (h n k) -> p h n k", h=H, k=k), src,
                                           level_mask(l), ALU.mult))
                sk.add("dve", f)

                if l:
                    def f(e, s, l=l, b=b, n=n):
                        need(e, e_Y, s, n - NB)
                        need(e, e_W, s, b) if l == 1 else need(e, e_Zp, s, n - 2 * NB)
                        e_Xs.by(e.transpose(X[:, b, :], Y[:, b, :]))
                    sk.add("dve", f)
            for b in range(NB):
                n = NB * l + b
                if l:
                    def f(e, s, l=l, b=b, n=n):
                        need(e, e_W, s, n)
                        need(e, e_Xs, s, n - NB)
                        for h in range(H):
                            i = e.matmul(cell[b][:, h * HP:(h + 1) * HP], X[:, b, hs(h)],
                                         Wm[:, b, h * HP:(h + 1) * HP], start=True, stop=True)
                        e_Zp.by(i)
                    sk.add("pe", f)

                if l == 0:
                    def f(e, s, b=b):
                        if b == 0:
                            need(e, e_Xp, s - 1)
                        e_Yo.by(e.tensor_tensor(
                            hv(Y, b).rearrange("p h (n k) -> p h n k", k=2)[:, :, :, 1],
                            mask(C_ID).rearrange("p h (n k) -> p h n k", k=2)[:, :, :, 1],
                            mask(C_ID).rearrange("p h (n k) -> p h n k", k=2)[:, :, :, 1], ALU.mult))
                    sk.add("pool", f)

                def f(e, s, l=l, b=b, n=n):
                    k = LEVELS[l]
                    yv = even(Y[:, b, :], k).rearrange("p (h n) k -> p h n k", h=H)
                    wv_ = Wm[:, b, :].rearrange("p (h n k) -> p h n k", h=H, k=k)
                    if l == 0:
                        need(e, e_W, s, n)
                        if b == 0:
                            need(e, e_Xp, s - 1)
                        idv = mask(C_ID).rearrange("p h (n k) -> p h n k", k=2)[:, :, :, 0:1]
                        need(e, e_Yo, s, b)
                        e_Y.by(e.tensor_tensor(yv, idv, wv_, ALU.subtract))
                    else:
                        need(e, e_Zp, s, n - NB)
                        e_Y.by(e.tensor_tensor(yv, yv, cell[b][:, 0:H * HP].rearrange(
                            "p (h n k) -> p h n k", h=H, k=k), ALU.subtract))
                sk.add("dve", f)

        sk.at("v tokens")
        for b in range(NB):
            token_major(b, 1)

            def f(e, s, b=b):
                need(e, e_tk, s, NB + b)
                need(e, e_nrm, s)
                need(e, e_a2, s - 1, b)
                need(e, e_so, s - 1, b)
                e_vn.by(e.tensor_tensor(hv(y, b), hv(vtok, b), wide(nrm[:, b, H:2 * H]), ALU.mult))
            sk.add("pool", f)

        sk.at("recurrence")
        for b in range(NB):
            m = NB * (NL - 1) + b

            def f(e, s, b=b, m=m):
                need(e, e_Y, s, m)
                need(e, e_tk, s) if b == 0 else need(e, e_X, s, 0)
                for h in range(H):
                    i = e.transpose(turn[:, hs(h)], Y[:, b, hs(h)], ident)
                e_Xp.by(i)
                need(e, e_S, s - 1, b)
                for h in range(H):
                    i = e.matmul(cell[b][:, hs(h)], kT[:, h, hs(b)], S[:, b, hs(h)], start=True, stop=True)
                e_KS.by(i)
            sk.add("pe", f)

            def f(e, s, b=b, m=m):
                need(e, e_Xp, s, b)
                need(e, e_Zp, s, m - NB)
                e_X.by(e.copy(X[:, b, :], turn[:, :]))
            sk.add("act", f)

            def f(e, s, b=b):
                need(e, e_KS, s, b)
                need(e, e_vn, s, b)
                e_y.by(e.tensor_tensor(y[:, b, :], y[:, b, :], cell[b][:, :], ALU.subtract))
            sk.add("dve", f)
        for b in range(NB):
            m = NB * (NL - 1) + b

            def f(e, s, b=b, m=m):
                need(e, e_y, s, b)
                need(e, e_X, s, b)
                for h in range(H):
                    i = e.matmul(cell[b][:, hs(h)], X[0:HP, b, hs(h)], y[0:HP, b, hs(h)], start=True, stop=True)
                e_Xy.by(i)
            sk.add("pe", f)

            def f(e, s, b=b):
                need(e, e_Xy, s, b)
                e_first.by(e.copy(y[0:HP, b, :], cell[b][0:HP, :]))
                need(e, e_KTu, s - 1, b)
                need(e, e_g, s)
                for h in range(H):
                    i = e.activation(u[0:HP, b, hs(h)], cell[b][0:HP, hs(h)], ACT.Copy, scale=g[0:HP, b, h:h + 1])
                e_uf.by(i)
            sk.add("act", f)

            def f(e, s, b=b):
                need(e, e_first, s, b)
                need(e, e_Bc, s, b - 1) if b else need(e, e_X, s)
                for h in range(H):
                    i = e.matmul(turn[:, hs(h)], Bm[0:HP, b, hs(h)], y[0:HP, b, hs(h)], start=True, stop=True)
                e_Bu.by(i)
            sk.add("pe", f)

            def f(e, s, b=b):
                need(e, e_Bu, s, b)
                e_Bc.by(e.tensor_tensor(y[HP:P, b, :], y[HP:P, b, :], turn[HP:P, :], ALU.subtract))
            sk.add("dve", f)

            def f(e, s, b=b):
                need(e, e_Bc, s, b)
                need(e, e_uf, s, b)
                for h in range(H):
                    i = e.matmul(cell[b][:, hs(h)], X[HP:P, b, hs(h)], y[HP:P, b, hs(h)], start=True, stop=True)
                e_all.by(i)
            sk.add("pe", f)

            def f(e, s, b=b):
                need(e, e_all, s, b)
                for h in range(H):
                    i = e.activation(u[HP:P, b, hs(h)], cell[b][HP:P, hs(h)], ACT.Copy, scale=g[HP:P, b, h:h + 1])
                e_u.by(i)
            sk.add("act", f)
        for b in range(NB):
            def f(e, s, b=b):
                need(e, e_u, s, b)
                need(e, e_aT, s, b)
                for h in range(H):
                    e.matmul(cell[b][:, hs(h)], qT[:, h, hs(b)], S[:, b, hs(h)], start=True, stop=False)
                    i = e.matmul(cell[b][:, hs(h)], aT[:, b, hs(h)], u[:, b, hs(h)], start=False, stop=True)
                e_o.by(i)
            sk.add("pe", f)

            def f(e, s, b=b):
                need(e, e_o, s, b)
                need(e, e_rn, s)
                need(e, e_on, s - 1, b)
                need(e, e_f2, s - 1)
                for h in range(H):
                    o, c = cell[b][:, hs(h)], rn[:, b, h:h + 1]
                    i = e.activation(dl[:, b, hs(h)], o, ACT.Copy, scale=c)
                e_dc.by(i)
                need(e, e_dc, s, b)
                for h in range(H):
                    o, c = cell[b][:, hs(h)], rn[:, b, h:h + 1]
                    i = e.activation(o, o, ACT.Abs, scale=c, accum_out=ft[:, b, H + h:H + h + 1])
                e_d.by(i)
            sk.add("act", f)
        for b in range(NB):
            def f(e, s, b=b):
                need(e, e_d, s, b)
                for h in range(H):
                    i = e.matmul(cell[b][:, hs(h)], ktok[:, b, hs(h)], u[:, b, hs(h)], start=True, stop=True)
                e_KTu.by(i)
            sk.add("pe", f)

            def f(e, s, b=b):
                need(e, e_KTu, s, b)
                e_S.by(e.tensor_tensor(S[:, b, :], S[:, b, :], cell[b][:, :], ALU.add))
            sk.add("dve", f)

        sk.at("mix in")

        def f(e, s):
            need(e, e_xcp, s)
            need(e, e_fmm, s - 1)
            need(e, e_r, s - 1)
            xrv = ka[:, :, :].rearrange("p c (b t) -> p c b t", b=NB)
            need(e, e_l, s - 1)
            need(e, e_kv, s - 1)
            e_dx.by(e.tensor_tensor(xrv, xsh[:, :, :, 1:1 + P], xsh[:, :, :, 0:P], ALU.subtract))
            need(e, e_dx, s)
            for j, dst in enumerate((xr, xk)):
                for c in range(CB):
                    e_xrk.by(e.scalar_tensor_tensor(
                        dst[:, c, :].rearrange("p (b t) -> p b t", b=NB), xrv[:, c, :, :],
                        mu[:, j, c:c + 1], xsh[:, c, :, 0:P], ALU.mult, ALU.add))
        sk.add("dve", f)

        sk.at("FFN")
        for pair in range(2):
            def f(e, s, pair=pair):
                need(e, e_xrk, s)
                need(e, e_xb, s - 1, pair)
                for c in range(2):
                    for k in range(CB):
                        i = e.matmul(dense[pair][:, c * W:(c + 1) * W], wfk[:, k, hs(2 * pair + c)], xk[:, k, :],
                                     start=(k == 0), stop=(k == CB - 1))
                e_fmm.by(i)
            sk.add("pe", f)

            def f(e, s, pair=pair):
                need(e, e_fmm, s, pair)
                need(e, e_ka, s, 0) if pair else need(e, e_ka, s - 1)
                e_frl.by(e.activation(rl[:, :], dense[pair][:, :], ACT.Relu))
            sk.add("act", f)

            def f(e, s, pair=pair):
                need(e, e_frl, s, pair)
                need(e, e_xrk, s)
                e_ka.by(e.activation(ka[:, 2 * pair:2 * pair + 2, :],
                                     rl[:, :].rearrange("p (c w) -> p c w", c=2), ACT.Square))
            sk.add("act", f)
        for b in range(NB):
            def f(e, s, b=b):
                need(e, e_xrk, s)
                need(e, e_frl, s, 0) if b == 0 else need(e, e_gate, s, 0)
                for k in range(CB):
                    i = e.matmul(dense[0][:, :], xr[:, k, hs(b)], wr[:, k, :], start=(k == 0), stop=(k == CB - 1))
                e_r.by(i)
                need(e, e_ka, s)
                need(e, e_frl, s, 1) if b == 0 else need(e, e_gate, s, 0)
                for k in range(CB):
                    i = e.matmul(dense[1][:, :], ka[:, k, hs(b)], wfv[:, k, :], start=(k == 0), stop=(k == CB - 1))
                e_kv.by(i)
            sk.add("pe", f)

            def f(e, s, b=b):
                need(e, e_r, s, b)
                need(e, e_res, s, 0) if b else need(e, e_res, s - 1, 1)
                e_th.by(e.activation(th[:, :], dense[0][:, :], ACT.Tanh, scale=0.5))
            sk.add("act", f)

            def f(e, s, b=b):
                need(e, e_th, s, b)
                need(e, e_kv, s, b)
                e_gate.by(e.scalar_tensor_tensor(th[:, :], th[:, :], 1.0, dense[1][:, :], ALU.add, ALU.mult))
            sk.add("dve", f)

            def f(e, s, b=b):
                need(e, e_gate, s, b)
                e.wait_ge(xb_in, s * 16 + 16)
                e_res.by(e.tensor_tensor(xb[:, b, :], xb[:, b, :], th[:, :], ALU.add))
            sk.add("pool", f)

        convs = [[] for _ in range(H)]
        for h in range(H):
            blocks = [((3 * h + p) // CB, (3 * h + p) % CB) for p in range(3)]
            sk.at("first taps")

            def f(e, s, h=h, blocks=blocks):
                if h == 0:
                    need(e, e_act, s)
                need(e, e_km, s - 1 if h < 2 else s, (h + 2) % H)
                for p, (j, c) in enumerate(blocks):
                    i = e.activation(my[h % 2][:, p, :].rearrange("p (b t) -> p b t", b=NB),
                                     vT[:, c, :, VH - TAPS[j] + 1:VH - TAPS[j] + 1 + P], ACT.Copy,
                                     scale=mw[:, WOFF[j] + c * TAPS[j]:WOFF[j] + c * TAPS[j] + 1])
                e_t0.by(i)
            sk.add("act", f)

            plan = sorted((t, p) for p in range(3) for t in range(1, TAPS[blocks[p][0]]))
            last = {}
            for t, p in plan:
                j, c = blocks[p]

                def f(e, s, h=h, t=t, p=p, j=j, c=c, last=last):
                    if t == 1:
                        need(e, e_t0, s, h)
                    o = my[h % 2][:, p, :].rearrange("p (b t) -> p b t", b=NB)
                    off = VH - (TAPS[j] - 1) + t
                    src = vT[:, c, :, off:off + P]
                    col = WOFF[j] + c * TAPS[j] + t
                    if t > 1:
                        chain.after(e, last[p])
                    i = e.scalar_tensor_tensor(o, src, mw[:, col:col + 1], o, ALU.mult, ALU.add)
                    if t < TAPS[j] - 1:
                        last[p] = chain.link(i)
                    else:
                        e_msc.by(i)
                convs[h].append(f)

        for h in range(H):
            sk.at("kernel mix")

            def f(e, s, h=h):
                need(e, e_msc, s, 3 * h + 2)
                if h:
                    need(e, e_ym, s, h - 1)
                else:
                    need(e, e_lb, s - 1)
                for p in range(3):
                    i = e.matmul(s_mix, km[:, p, :], my[h % 2][:, p, :], start=(p == 0), stop=(p == 2))
                e_km.by(i)
            sk.add("pe", f)

            def f(e, s, h=h):
                need(e, e_km, s, h)
                if h == 0:
                    need(e, e_cm, s - 1)
                e_ym.by(e.copy(ym[:, h, :], s_mix))
            sk.add("act", f)

        sc.at("channel mix")
        for b in range(NB):
            def f(e, s, b=b):
                need(e, e_ym, s)
                need(e, (e_th, e_gate)[b], s)
                for k in range(CB):
                    i = e.matmul(dense[b][:, :], ym[:, k, hs(b)], cm[:, k, :], start=(k == 0), stop=(k == CB - 1))
                e_cm.by(i)
            sc.add("pe", f)

            def f(e, s, b=b):
                need(e, e_cm, s, b)
                need(e, e_a1, s - 1, b)
                need(e, e_f2, s - 1)
                e_msb.by(e.copy(ms[:, b, :], dense[b][:, :]))
                need(e, e_msb, s, b)
                for h in range(H):
                    i = e.activation(dense[b][:, hs(h)], dense[b][:, hs(h)], ACT.Abs, accum_out=ft[:, b, h:h + 1])
                e_ms.by(i)
            sc.add("act", f)

        def part(i):
            return fparts[:, :, :, i, :]

        def over(t):
            return t[:, :, None, :].broadcast_to([P, NB, PARTS, NF])

        def f(e, s):
            need(e, e_ms, s)
            need(e, e_d, s)
            need(e, e_tk, s)
            need(e, e_fp, s - 1)
            e_f1.by(e.copy(part(0), over(ft)))
        sc.add("act", f)

        def f(e, s):
            need(e, e_f1, s)
            need(e, e_f4, s - 1)
            e_f2.by(e.tensor_tensor(frest[:, :, :], ft[:, :, :], fparts[:, :, 0, 0, :], ALU.subtract))
        sc.add("dve", f)

        def f(e, s):
            need(e, e_f2, s)
            need(e, e_f4, s - 1)
            need(e, e_fp, s - 1)
            e_f3.by(e.copy(part(1), over(frest)))
        sc.add("act", f)

        def f(e, s):
            need(e, e_f3, s)
            need(e, e_fp, s - 1)
            e_f4.by(e.tensor_tensor(part(2), over(frest), part(1), ALU.subtract))
        sc.add("dve", f)

        def f(e, s):
            need(e, e_f4, s)
            need(e, e_ym, s)
            for b in range(NB):
                e_fp.by(e.matmul(s_ft[:, hs(b)], fparts[:, b, :, :, :].rearrange("p j i n -> p (j i n)"),
                                 ident16[:, :], start=True, stop=True))
        sc.add("pe", f)

        def f(e, s):
            need(e, e_fp, s)
            need(e, e_z, s - 1)
            for b in range(NB):
                e_fT.by(e.activation(ftT[:, hs(b)], s_ft[:, hs(b)], ACT.Copy, scale=1.0 / P))
        sc.add("act", f)

        sc.at("fusion")
        for pair in range(HB // 2):
            def f(e, s, pair=pair):
                if pair < 2:
                    need(e, e_ms, s, pair)
                else:
                    need(e, e_h, s, pair - 2)
                for c in range(2):
                    o = dense[pair % 2][:, c * W:(c + 1) * W]
                    for k in range(CB):
                        e.matmul(o.rearrange("p (b t) -> p b t", b=NB), w1[:, k, hs(2 * pair + c)],
                                 xsh[:, k, :, 1:1 + P], start=(k == 0), stop=False)
                    need(e, e_fT, s)
                    i = e.matmul(o, w1x[:, hs(2 * pair + c)], ftT[:, :], start=False, stop=True)
                e_z.by(i)
            sc.add("pe", f)

            def f(e, s, pair=pair):
                need(e, e_z, s, pair)
                need(e, e_r, s)
                need(e, e_fmm, s)
                for c in range(2):
                    m = 2 * pair + c
                    i = e.activation(hd[m], dense[pair % 2][:, c * W:(c + 1) * W], ACT.Gelu,
                                     bias=b1[:, m:m + 1])
                e_h.by(i)
            sc.add("act", f)

        def logits(pair):
            def f(e, s):
                need(e, e_fT, s)
                need(e, e_h, s, pair)
                for c in range(2):
                    m = 2 * pair + c
                    for b in range(NB):
                        i = e.matmul(s_lg[:, b * NF:(b + 1) * NF], hd[m][:, hs(b)], w2[:, m, :],
                                     start=(m == 0 and b == 0), stop=(m == HB - 1), skip_group_check=True)
                e_l.by(i)
            return f
        for pair in range(HB // 2):
            sc.add("pe", logits(pair))

        sc.at("softmax")
        l3 = lg[:, :, :, :].rearrange("p b h r -> p (b h) r")
        w3 = gw[:, :, :, :].rearrange("p b h r -> p (b h) r")

        def f(e, s):
            need(e, e_l, s)
            need(e, e_gw, s - 1)
            e_lb.by(e.tensor_tensor(lg[:, :, :, :].rearrange("p b h r -> p b (h r)"),
                                    s_lg.rearrange("p (b n) -> p b n", b=NB),
                                    b2[:, None, :].broadcast_to([P, NB, NF]), ALU.add))
        sc.add("dve", f)

        def f(e, s):
            need(e, e_lb, s)
            e_mx.by(e.tensor_reduce(mx[:, :], l3, AX.X, ALU.max))
        sc.add("dve", f)

        def f(e, s):
            need(e, e_mx, s)
            e_sub.by(e.tensor_tensor(l3, l3, mx[:, :, None].broadcast_to([P, NB * H, 3]), ALU.subtract))
        sc.add("dve", f)

        def f(e, s):
            need(e, e_ex, s)
            e_sm.by(e.tensor_reduce(sm[:, :], l3, AX.X, ALU.add))
        sc.add("dve", f)

        def f(e, s):
            need(e, e_sm, s)
            e_rs.by(e.reciprocal(rs[:, :], sm[:, :]))
        sc.add("dve", f)

        def f(e, s):
            need(e, e_rs, s)
            need(e, e_m0, s - 1)
            need(e, e_m1, s - 1)
            need(e, e_m2, s - 1)
            e_gw.by(e.tensor_tensor(w3, l3, rs[:, :, None].broadcast_to([P, NB * H, 3]), ALU.mult))
        sc.add("dve", f)

        def f(e, s):
            need(e, e_sub, s)
            e_ex.by(e.activation(lg[:, :, :, :], lg[:, :, :, :], ACT.Exp))
        sc.add("act", f)

        sc.at("out")
        for b in range(NB):
            def f(e, s, b=b):
                need(e, e_gw, s)
                need(e, e_ms, s, b)
                need(e, e_tk, s, NB + b)
                need(e, e_all, s, b)
                e_m2.by(e.tensor_tensor(hv(y, b), hv(vtok, b), wide(gw[:, b, :, 2]), ALU.mult))
                e_m0.by(e.tensor_tensor(hv(ms, b), hv(ms, b), wide(gw[:, b, :, 0]), ALU.mult))
            sc.add("pool", f)

            def f(e, s, b=b):
                need(e, e_gw, s)
                need(e, e_d, s, b)
                for h in range(H):
                    i = e.activation(dl[:, b, hs(h)], dl[:, b, hs(h)], ACT.Copy, scale=gw[:, b, h, 1:2])
                e_m1.by(i)
            sc.add("act", f)

            def f(e, s, b=b):
                need(e, e_m1, s, b)
                need(e, e_m0, s, b)
                e_a1.by(e.tensor_tensor(dl[:, b, :], dl[:, b, :], ms[:, b, :], ALU.add))
            sc.add("dve", f)

            def f(e, s, b=b):
                need(e, e_a1, s, b)
                need(e, e_m2, s, b)
                e_a2.by(e.tensor_tensor(dl[:, b, :], dl[:, b, :], y[:, b, :], ALU.add))
            sc.add("dve", f)

            def f(e, s, b=b):
                need(e, e_a2, s, b)
                need(e, e_ro, s - 1, b)
                for h in range(H):
                    i = e.activation(y[:, b, hs(h)], dl[:, b, hs(h)], ACT.Square, accum_out=so[:, b, h:h + 1])
                e_so.by(i)
            sc.add("act", f)

            def f(e, s, b=b):
                need(e, e_so, s, b)
                need(e, e_rro, s - 1, b)
                e_ro.by(e.activation(ro[:, b, :], so[:, b, :], ACT.Sqrt, bias=eps[:, 2:3], scale=1.0 / P))
            sc.add("act", f)

            def f(e, s, b=b):
                need(e, e_ro, s, b)
                e_rro.by(e.reciprocal(rro[:, b, :], ro[:, b, :]))
            sc.add("dve", f)

            def f(e, s, b=b):
                need(e, e_rro, s, b)
                for h in range(H):
                    i = e.activation(dl[:, b, hs(h)], dl[:, b, hs(h)], ACT.Copy, scale=rro[:, b, h:h + 1])
                e_on.by(i)
            sc.add("act", f)

            def f(e, s, b=b):
                need(e, e_on, s, b)
                need(e, e_h, s, HB // 2 - 2 + b)
                for h in range(H):
                    i = e.transpose(dense[b][:, hs(h)], dl[:, b, hs(h)], ident)
                e_oTp.by(i)
            sc.add("pe", f)

            def f(e, s, b=b):
                need(e, e_oTp, s, b)
                need(e, e_att, s - 1)
                e_oT.by(e.copy(oT[:, :, hs(b)], bh(dense[b])))
            sc.add("act", f)

            def f(e, s, b=b):
                need(e, e_oT, s, b)
                for h in range(H):
                    i = e.matmul(dense[b][:, :], oT[:, h, hs(b)], wo[:, h, :], start=(h == 0), stop=(h == H - 1))
                e_att.by(i)
            sc.add("pe", f)

            def f(e, s, b=b):
                need(e, e_att, s, b)
                need(e, e_res, s, b)
                e_xb.by(e.tensor_tensor(xb[:, b, :], xb[:, b, :], dense[b][:, :], ALU.add))
            sc.add("dve", f)

        def f(e, s):
            need(e, e_xb, s)
            e.dma_start(out[:, bass.ds(s * P, P), :].rearrange("b p d -> p b d"), xb[:, :, :]).then_inc(stored, 16)
        sc.add("sp", f)

        sk.at("taps")
        tail = max(TAPS) - sorted(TAPS)[-2]
        body, fill = convs[2][:-tail], convs[3][:2 * tail]
        woven = [f for n in range(tail) for f in (convs[2][len(body) + n], *fill[2 * n:2 * n + 2])]
        for f in convs[0] + convs[1] + body + woven + convs[3][2 * tail:]:
            sk.add("dve", f)

        front_loads = [
            (cst[:, :], w["cst"]),
            (wq[:, :, :], w["wq"].rearrange("(k p) n -> p k n", p=P)),
            (wk[:, :, :], w["wk"].rearrange("(k p) n -> p k n", p=P)),
        ]
        for j, n in enumerate(("cq", "ck", "cv")):
            front_loads.append((cw[:, j, :, :], w[n].rearrange("(c p) k -> p c k", p=P)))
        front_loads += [
            (wv[:, :, :], w["wv"].rearrange("(k p) n -> p k n", p=P)),
            (wb[:, :, :], w["wb"].rearrange("(k p) n -> p k n", p=P)),
        ]
        loads = [
            (wr[:, :, :], w["wrT"].rearrange("(k p) n -> p k n", p=P)),
            (wfk[:, :, :], w["wfkT"].rearrange("(k p) n -> p k n", p=P)),
            (wfv[:, :, :], w["wfvT"].rearrange("(k p) n -> p k n", p=P)),
            (cm[:, :, :], w["cm"].rearrange("(k p) n -> p k n", p=P)),
            (wo[:, :, :], w["wo"].rearrange("(k p) n -> p k n", p=P)),
            (w1[:, :, :], w["w1"][0:D, :].rearrange("(k p) n -> p k n", p=P)),
            (km[:, :, :], w["km"].rearrange("(k p) n -> p k n", p=P)),
            (w2[:, :, :], w["w2"].rearrange("(k p) n -> p k n", p=P)),
            (b1[:, :], w["b1"]),
            (b2[:, :], w["b2"][None, :].broadcast_to([P, NF])),
            (onw[:, :], w["onw"].rearrange("(p a) -> p a", a=1)),
            (mu[:, 0, :], w["mu_r"]),
            (mu[:, 1, :], w["mu_k"]),
        ]
        for j, t in enumerate(TAPS):
            loads.append((mw[:, WOFF[j]:WOFF[j] + CB * t].rearrange("p (c k) -> p c k", k=t),
                          w[f"m{t}"].rearrange("(c p) k -> p c k", p=P)))
        rows = xr[:, :, :].rearrange("p c w -> p (c w)")
        for i in range(PARTS * PARTS):
            loads.append((rows[i * NF:(i + 1) * NF, :], w["w1"][D:D + NF, :]))
        NSET = 7

        def start_load(e, part, sem):
            for dst, src in part:
                e.dma_start(dst, src).then_inc(sem, 16)

        def start_pool(e):
            for t in (S[:, :, :], halo[:, :, :, :], vT[:, :, :, :], xsh[:, :, :, :]):
                e.memset(t, 0.0).then_inc(setup, 1)
            for i, v in enumerate((1e-5, 1e-6, 1e-5)):
                e.memset(eps[:, i:i + 1], v).then_inc(setup, 1)

        def start_dve(e):
            done = 0

            def then(ins):
                nonlocal done
                done += 1
                ins.then_inc(scaled, 1)
                e.wait_ge(scaled, done)

            then(e.tensor_scalar(wfv[:, :, :], wfv[:, :, :], 0.5, None, ALU.mult))
            for k in range(CB):
                then(e.tensor_scalar(wo[:, k, :], wo[:, k, :], onw[:, 0:1], None, ALU.mult))
            then(e.tensor_copy(ident16[:, :], ident))
            whole, rest, chosen = (t[0:NROW, :, :].rearrange("p c w -> p (c w)") for t in (xr, xk, ka))
            for j in range(PARTS):
                pick = cst[0:NROW, C_PART + j:C_PART + j + 1]
                then(e.tensor_copy(w1x[:, :], (rest if j else whole)))
                if j == 0:
                    then(e.tensor_scalar(chosen, w1x[:, :], pick, None, ALU.mult))
                else:
                    then(e.scalar_tensor_tensor(chosen, w1x[:, :], pick, chosen, ALU.mult, ALU.add))
                then(e.tensor_tensor(rest, (rest if j else whole), w1x[:, :], ALU.subtract))
            then(e.tensor_copy(w1x[:, :], chosen))

        order = {k: sorted(sf.order(k) + sk.order(k) + sc.order(k), key=lambda t: (t[0], -t[1]))
                 for k in ("pe", "act", "dve", "pool", "sp")}

        def program(e, k):
            if k == "sp":
                start_load(e, front_loads, front_loaded)
            e.wait_ge(setup, NSET)
            if k != "sp":
                e.wait_ge(front_loaded, 16 * len(front_loads))

            def iteration(i, ages):
                if k == "dve":
                    chain.restart(e, isinstance(i, int) and i == 0)
                for _, age, fn in order[k]:
                    if age in ages:
                        fn(e, i - age)

            iteration(0, (0,))
            if k == "sp":
                start_load(e, loads, loaded)
            else:
                e.wait_ge(loaded, 16 * len(loads))
            if k == "dve":
                start_dve(e)
            if k in ("pe", "act"):
                e.wait_ge(scaled, 2 + CB + 3 * PARTS + 1)
            iteration(1, (0, 1))
            iteration(2, (0, 1, 2))
            with e.Fori(3, NS) as i:
                iteration(i, (0, 1, 2))
            iteration(NS, (1, 2))
            iteration(NS + 1, (2,))
            if k == "sp":
                e.wait_ge(stored, 16 * NS)

        block = ctx.enter_context(nc.Block())

        @block.sync
        def _(e):
            program(e, "sp")

        @block.gpsimd
        def _(e):
            start_pool(e)
            program(e, "pool")

        @block.vector
        def _(e):
            program(e, "dve")

        @block.scalar
        def _(e):
            program(e, "act")

        @block.tensor
        def _(e):
            program(e, "pe")

        for name, ev in events:
            assert ev.seen == 4 * ev.n, (name, ev.seen, ev.n)


def kernel(**inputs):
    import numpy as np
    import concourse.bacc as bacc
    from concourse.bass_utils import run_bass_kernel_spmd

    cst = np.zeros((P, C_ONE + 2), np.float32)
    r, c = np.arange(P)[:, None], np.arange(P)[None, :]
    cst[:, C_UP * P:(C_UP + 1) * P] = r < c
    cst[:, C_UPI * P:(C_UPI + 1) * P] = r <= c
    cst[:, C_ID * P:(C_ID + 1) * P] = r == c
    for i, k in enumerate(LEVELS):
        n = np.arange(HP)[None, :] // k
        cst[:, C_LEV + i * HP:C_LEV + (i + 1) * HP] = (r // (2 * k) == n) & (r // k % 2 == 1)
    for j in range(PARTS):
        cst[j * PARTS * NF:(j + 1) * PARTS * NF, C_PART + j] = 1.0
    cst[:, C_ONE:] = 1.0

    a = {k: np.asarray(v) for k, v in inputs.items()}
    A = "L0_attn_"
    arrays = {
        "x": a[A + "hidden_states"], "wq": a[A + "Wq"], "wk": a[A + "Wk"], "wv": a[A + "Wv"], "wb": a[A + "Wb"],
        "cq": a[A + "conv_q_w"], "ck": a[A + "conv_k_w"], "cv": a[A + "conv_v_w"],
        "m3": a[A + "ms_w3"], "m15": a[A + "ms_w15"], "m31": a[A + "ms_w31"],
        "km": a[A + "kernel_mix_w"], "cm": a[A + "channel_mixer_w"],
        "w1": a[A + "fusion_w1"], "b1": a[A + "fusion_b1"].reshape(HB, P).T, "w2": a[A + "fusion_w2"],
        "b2": a[A + "fusion_b2"],
        "onw": a[A + "o_norm_w"], "wo": a[A + "Wo"],
        "wrT": a["L0_ffn_W_r"].T, "wfkT": a["L0_ffn_W_k"].T, "wfvT": a["L0_ffn_W_v"].T,
        "mu_r": a["L0_ffn_mu_r"].reshape(CB, P).T, "mu_k": a["L0_ffn_mu_k"].reshape(CB, P).T, "cst": cst,
    }
    arrays = {k: np.ascontiguousarray(v) for k, v in arrays.items()}
    nc = bacc.Bacc("TRN2", target_bir_lowering=False, num_devices=1)
    arrays = {f"in_{k}": v for k, v in arrays.items()}
    aps = {k[3:]: nc.dram_tensor(k, v.shape, F32, kind="ExternalInput").ap() for k, v in arrays.items()}
    out = nc.dram_tensor("out", arrays["in_x"].shape, F32, kind="ExternalOutput").ap()
    x = aps.pop("x")
    build(nc, x, out, aps)
    r = run_bass_kernel_spmd(nc, [arrays], core_ids=[0])
    return r.results[0]["out"]
```
